# Optimizing a Trainium2 kernel written in Bass

```python
import numpy as np
import jax
import jax.numpy as jnp

def _softmax(x, axis=-1):
    return jax.nn.softmax(x, axis=axis)

def _gelu(x):
    return jax.nn.gelu(x, approximate=True)

def _silu(x):
    return jax.nn.silu(x)

def _sigmoid(x):
    return jax.nn.sigmoid(x)

def _layernorm(x, axis=-1, eps=1e-05):
    m = jnp.mean(x, axis=axis, keepdims=True)
    v = jnp.var(x, axis=axis, keepdims=True)
    return (x - m) / jnp.sqrt(v + eps)

def _scatter_add(tgt, idx, src, axis=0):
    return tgt.at[idx].add(src)

def _segment_sum(src, seg, n):
    return jax.ops.segment_sum(src, seg, n)
kernel_name = 'mk_macaron_d1_jaxref_r8_9aa959'

def setup_inputs(seed: int=0):
    np.random.seed(seed)
    _w = jnp.asarray

    def _L0_attn_setup():
        import jax, jax.numpy as jnp
        import numpy as np
        D_MODEL = 128
        N_HEAD = 16
        N_KV_HEAD = 4
        HEAD_DIM = D_MODEL // N_HEAD
        N_GROUP = N_HEAD // N_KV_HEAD
        ROPE_BASE = 10000.0
        ROPE_DIM = HEAD_DIM

        def _rope_tables(seq_len, dtype):
            half = ROPE_DIM // 2
            inv_freq = 1.0 / ROPE_BASE ** (jnp.arange(0, half, dtype=jnp.float32) * 2.0 / ROPE_DIM)
            pos = jnp.arange(seq_len, dtype=jnp.float32)
            freqs = pos[:, None] * inv_freq[None, :]
            return (jnp.cos(freqs).astype(dtype), jnp.sin(freqs).astype(dtype))

        def _apply_rope(t):
            S = t.shape[2]
            cos, sin = _rope_tables(S, t.dtype)
            half = ROPE_DIM // 2
            t1 = t[..., :half]
            t2 = t[..., half:ROPE_DIM]
            rot = jnp.concatenate([t1 * cos - t2 * sin, t1 * sin + t2 * cos], axis=-1)
            if ROPE_DIM < t.shape[-1]:
                rot = jnp.concatenate([rot, t[..., ROPE_DIM:]], axis=-1)
            return rot
        key = jax.random.key(seed)
        ks = jax.random.split(key, 5)
        B, S = (1, 512)
        sd = 1.0 / np.sqrt(D_MODEL)
        x = jax.random.normal(ks[0], (B, S, D_MODEL), dtype=jnp.float32)
        w_q = jax.random.normal(ks[1], (D_MODEL, N_HEAD * HEAD_DIM), dtype=jnp.float32) * sd
        w_k = jax.random.normal(ks[2], (D_MODEL, N_KV_HEAD * HEAD_DIM), dtype=jnp.float32) * sd
        w_v = jax.random.normal(ks[3], (D_MODEL, N_KV_HEAD * HEAD_DIM), dtype=jnp.float32) * sd
        w_o = jax.random.normal(ks[4], (D_MODEL, D_MODEL), dtype=jnp.float32) * sd
        return {'x': x, 'w_q': w_q, 'w_k': w_k, 'w_v': w_v, 'w_o': w_o}
    _L0_attn_in = _L0_attn_setup()

    def _L0_ffn_setup():
        import jax, jax.numpy as jnp
        import numpy as np
        B, N, D, H, E = (4, 128, 128, 16, 8)
        DK = D // H
        HID = 4 * D
        EPS = 1e-05

        def _layernorm(x, w, b):
            m = jnp.mean(x, axis=-1, keepdims=True)
            v = jnp.mean(jnp.square(x - m), axis=-1, keepdims=True)
            return (x - m) * jax.lax.rsqrt(v + EPS) * w + b

        def _msa(x, w_qkv, w_proj):
            b, n, d = x.shape
            qkv = (x @ w_qkv).reshape(b, n, 3, H, DK)
            q = qkv[:, :, 0].transpose(0, 2, 1, 3)
            k = qkv[:, :, 1].transpose(0, 2, 1, 3)
            v = qkv[:, :, 2].transpose(0, 2, 1, 3)
            attn = jnp.einsum('bhnd,bhmd->bhnm', q, k) * (1.0 / np.sqrt(DK))
            attn = jax.nn.softmax(attn, axis=-1)
            y = jnp.einsum('bhnm,bhmd->bhnd', attn, v)
            y = y.transpose(0, 2, 1, 3).reshape(b, n, d)
            return y @ w_proj

        def _moe_mlp(x, gate_w, gate_b, w1, w2):
            b, n, d = x.shape
            xf = x.reshape(b * n, d)
            logits = xf @ gate_w + gate_b
            one_hot = jax.nn.one_hot(jnp.argmax(logits, axis=-1), E, dtype=xf.dtype)
            h = jax.nn.gelu(jnp.einsum('td,edh->teh', xf, w1), approximate=True)
            y = jnp.einsum('teh,ehd->ted', h, w2)
            out = jnp.einsum('te,ted->td', one_hot, y)
            return out.reshape(b, n, d)
        key = jax.random.key(seed)
        ks = jax.random.split(key, 8)
        s = 0.02
        return {'x': jax.random.normal(ks[0], (B, N, D), jnp.float32), 'ln1_w': jnp.ones((D,), jnp.float32), 'ln1_b': jnp.zeros((D,), jnp.float32), 'w_qkv': jax.random.normal(ks[1], (D, 3 * D), jnp.float32) * s, 'w_proj': jax.random.normal(ks[2], (D, D), jnp.float32) * s, 'ln2_w': jnp.ones((D,), jnp.float32), 'ln2_b': jnp.zeros((D,), jnp.float32), 'gate_w': jax.random.normal(ks[3], (D, E), jnp.float32) * s, 'gate_b': jnp.zeros((E,), jnp.float32), 'w1': jax.random.normal(ks[4], (E, D, HID), jnp.float32) * s, 'w2': jax.random.normal(ks[5], (E, HID, D), jnp.float32) * s}
    _L0_ffn_in = _L0_ffn_setup()
    _d = {'L0_attn_x': _L0_attn_in['x'], 'L0_attn_w_q': _L0_attn_in['w_q'], 'L0_attn_w_k': _L0_attn_in['w_k'], 'L0_attn_w_v': _L0_attn_in['w_v'], 'L0_attn_w_o': _L0_attn_in['w_o'], 'L0_ffn_ln1_w': _L0_ffn_in['ln1_w'], 'L0_ffn_ln1_b': _L0_ffn_in['ln1_b'], 'L0_ffn_w_qkv': _L0_ffn_in['w_qkv'], 'L0_ffn_w_proj': _L0_ffn_in['w_proj'], 'L0_ffn_ln2_w': _L0_ffn_in['ln2_w'], 'L0_ffn_ln2_b': _L0_ffn_in['ln2_b'], 'L0_ffn_gate_w': _L0_ffn_in['gate_w'], 'L0_ffn_gate_b': _L0_ffn_in['gate_b'], 'L0_ffn_w1': _L0_ffn_in['w1'], 'L0_ffn_w2': _L0_ffn_in['w2']}
    _x0 = _d['L0_attn_x']
    _d['L0_attn_x'] = jax.random.normal(jax.random.fold_in(jax.random.key(seed), 1), (8, 512, 128), dtype=_x0.dtype)
    del _x0
    return _d

def reference(L0_attn_x, L0_attn_w_q, L0_attn_w_k, L0_attn_w_v, L0_attn_w_o, L0_ffn_ln1_w, L0_ffn_ln1_b, L0_ffn_w_qkv, L0_ffn_w_proj, L0_ffn_ln2_w, L0_ffn_ln2_b, L0_ffn_gate_w, L0_ffn_gate_b, L0_ffn_w1, L0_ffn_w2):

    def _L0_attn_ref(x, w_q, w_k, w_v, w_o):
        import jax, jax.numpy as jnp
        import numpy as np
        D_MODEL = 128
        N_HEAD = 16
        N_KV_HEAD = 4
        HEAD_DIM = D_MODEL // N_HEAD
        N_GROUP = N_HEAD // N_KV_HEAD
        ROPE_BASE = 10000.0
        ROPE_DIM = HEAD_DIM

        def _rope_tables(seq_len, dtype):
            half = ROPE_DIM // 2
            inv_freq = 1.0 / ROPE_BASE ** (jnp.arange(0, half, dtype=jnp.float32) * 2.0 / ROPE_DIM)
            pos = jnp.arange(seq_len, dtype=jnp.float32)
            freqs = pos[:, None] * inv_freq[None, :]
            return (jnp.cos(freqs).astype(dtype), jnp.sin(freqs).astype(dtype))

        def _apply_rope(t):
            S = t.shape[2]
            cos, sin = _rope_tables(S, t.dtype)
            half = ROPE_DIM // 2
            t1 = t[..., :half]
            t2 = t[..., half:ROPE_DIM]
            rot = jnp.concatenate([t1 * cos - t2 * sin, t1 * sin + t2 * cos], axis=-1)
            if ROPE_DIM < t.shape[-1]:
                rot = jnp.concatenate([rot, t[..., ROPE_DIM:]], axis=-1)
            return rot
        B, S, _ = x.shape
        q = (x @ w_q).reshape(B, S, N_HEAD, HEAD_DIM).transpose(0, 2, 1, 3)
        k = (x @ w_k).reshape(B, S, N_KV_HEAD, HEAD_DIM).transpose(0, 2, 1, 3)
        v = (x @ w_v).reshape(B, S, N_KV_HEAD, HEAD_DIM).transpose(0, 2, 1, 3)
        q = _apply_rope(q)
        k = _apply_rope(k)
        k = jnp.repeat(k, N_GROUP, axis=1)
        v = jnp.repeat(v, N_GROUP, axis=1)
        scale = 1.0 / jnp.sqrt(jnp.asarray(HEAD_DIM, dtype=x.dtype))
        scores = jnp.einsum('bhqd,bhkd->bhqk', q, k) * scale
        attn = jax.nn.softmax(scores, axis=-1)
        out = jnp.einsum('bhqk,bhkd->bhqd', attn, v)
        out = out.transpose(0, 2, 1, 3).reshape(B, S, D_MODEL)
        return out @ w_o

    def _L0_ffn_ref(x, ln1_w, ln1_b, w_qkv, w_proj, ln2_w, ln2_b, gate_w, gate_b, w1, w2):
        import jax, jax.numpy as jnp
        import numpy as np
        B, N, D, H, E = (4, 128, 128, 16, 8)
        DK = D // H
        HID = 4 * D
        EPS = 1e-05

        def _layernorm(x, w, b):
            m = jnp.mean(x, axis=-1, keepdims=True)
            v = jnp.mean(jnp.square(x - m), axis=-1, keepdims=True)
            return (x - m) * jax.lax.rsqrt(v + EPS) * w + b

        def _msa(x, w_qkv, w_proj):
            b, n, d = x.shape
            qkv = (x @ w_qkv).reshape(b, n, 3, H, DK)
            q = qkv[:, :, 0].transpose(0, 2, 1, 3)
            k = qkv[:, :, 1].transpose(0, 2, 1, 3)
            v = qkv[:, :, 2].transpose(0, 2, 1, 3)
            attn = jnp.einsum('bhnd,bhmd->bhnm', q, k) * (1.0 / np.sqrt(DK))
            attn = jax.nn.softmax(attn, axis=-1)
            y = jnp.einsum('bhnm,bhmd->bhnd', attn, v)
            y = y.transpose(0, 2, 1, 3).reshape(b, n, d)
            return y @ w_proj

        def _moe_mlp(x, gate_w, gate_b, w1, w2):
            b, n, d = x.shape
            xf = x.reshape(b * n, d)
            logits = xf @ gate_w + gate_b
            one_hot = jax.nn.one_hot(jnp.argmax(logits, axis=-1), E, dtype=xf.dtype)
            h = jax.nn.gelu(jnp.einsum('td,edh->teh', xf, w1), approximate=True)
            y = jnp.einsum('teh,ehd->ted', h, w2)
            out = jnp.einsum('te,ted->td', one_hot, y)
            return out.reshape(b, n, d)
        x = x + _msa(_layernorm(x, ln1_w, ln1_b), w_qkv, w_proj)
        x = x + _moe_mlp(_layernorm(x, ln2_w, ln2_b), gate_w, gate_b, w1, w2)
        return x
    x = L0_attn_x
    x = x + 0.5 * _L0_ffn_ref(_layernorm(x, axis=-1), L0_ffn_ln1_w, L0_ffn_ln1_b, L0_ffn_w_qkv, L0_ffn_w_proj, L0_ffn_ln2_w, L0_ffn_ln2_b, L0_ffn_gate_w, L0_ffn_gate_b, L0_ffn_w1, L0_ffn_w2)
    x = x + _L0_attn_ref(_layernorm(x, axis=-1), L0_attn_w_q, L0_attn_w_k, L0_attn_w_v, L0_attn_w_o)
    x = x + 0.5 * _L0_ffn_ref(_layernorm(x, axis=-1), L0_ffn_ln1_w, L0_ffn_ln1_b, L0_ffn_w_qkv, L0_ffn_w_proj, L0_ffn_ln2_w, L0_ffn_ln2_b, L0_ffn_gate_w, L0_ffn_gate_b, L0_ffn_w1, L0_ffn_w2)
    return x

_drawn_inputs = setup_inputs


def setup_inputs(seed=0):
    import zlib

    import numpy as np

    out = dict(_drawn_inputs(seed))
    spreads = {'L0_ffn_ln1_w': (1.0, 0.6),
     'L0_ffn_ln1_b': (0.0, 0.8),
     'L0_ffn_ln2_w': (1.0, 0.6),
     'L0_ffn_ln2_b': (0.0, 2.0),
     'L0_ffn_gate_b': (0.0, 0.295)}
    factors = {'L0_ffn_w_qkv': 8.0, 'L0_ffn_w_proj': 8.0}
    for name, (base, spread) in spreads.items():
        noise = np.random.default_rng([zlib.crc32(name.encode()), seed]).standard_normal(out[name].shape)
        drawn = base * np.exp(spread * noise) if base else spread * noise
        out[name] = jnp.asarray(drawn.astype(out[name].dtype))
    for name, factor in factors.items():
        out[name] = (out[name] * factor).astype(out[name].dtype)
    return out
```

```python
from collections import namedtuple
from contextlib import ExitStack

import numpy as np
import concourse.bass as bass
from concourse import mybir

F32 = mybir.dt.float32
F32R = mybir.dt.float32r
U32 = mybir.dt.uint32
ALU = mybir.AluOpType
ACT = mybir.ActivationFunctionType
AX = mybir.AxisListType

P = 128
B, S, D = 8, 512, 128
H, HD = 16, 8
QT = S // P
NT = B * QT
G, J = 4, 4
NG = B * G
KV = 4
E, HID = 8, 512
HT = HID // P
V1 = HD + 1
NBLK = NT + E
EPS = 1e-5
SCALE = float(1.0 / np.sqrt(HD))
MROW = 32
SLOT = J * S


def wait(eng, sem, value):
    if isinstance(value, int) and value <= 0:
        return
    eng.wait_ge(sem, value)


def batches(eng, body):
    body(0)
    with eng.Fori(1, B - 1) as b:
        body(b)
    body(B - 1)


def cols(tile, start, n):
    return tile[:, bass.ds(start, n)]


class Core:
    pass


def sems(ctx, nc, tag, names):
    handles, fields, values = [], [], []
    for entry in names.split():
        name, _, n = entry.partition(":")
        new = [nc.alloc_semaphore(name=f"{tag}_{name}{i}") for i in range(int(n or 1))]
        handles += new
        fields.append(name)
        values.append(new if n else new[0])

    def clear():
        nc.clear_and_free_semaphores(handles)
        nc.all_engine_barrier()

    ctx.callback(clear)
    return namedtuple("Sems", fields)(*values)




def layer_norm(dve, c, s, value, src, dst, var_ready, std_ready, count):
    nc = c.nc
    dve.sem_inc(s.held, 1)
    for t in range(QT):
        ins = nc.vector.bn_stats(c.stats[:, t, :], src(t))
    ins.then_inc(s.ln, 1)
    dve.wait_ge(s.ln, value + 1)
    dve.sem_inc(s.held, 1)
    for t in range(QT):
        ins = nc.vector.bn_aggr(c.moments[:, t, :], c.stats[:, t, :])
    ins.then_inc(s.ln, 1)
    dve.wait_ge(s.ln, value + 2)
    nc.vector.tensor_scalar(c.vareps[:, :], c.moments[:, :, 1], EPS, None, ALU.add).then_inc(var_ready, 1)
    dve.wait_ge(std_ready, count + 1)
    nc.vector.reciprocal(c.rstd[:, :], c.std[:, :]).then_inc(s.ln, 1)
    dve.wait_ge(s.ln, value + 3)
    for t in range(QT):
        ins = nc.vector.tensor_scalar(dst(t), src(t), c.moments[:, t, 0:1], c.rstd[:, t:t + 1],
                                      ALU.subtract, ALU.mult)
    ins.then_inc(s.ln, 1)
    dve.wait_ge(s.ln, value + 4)


def square_root(act, c, var_ready, std_ready, count):
    act.wait_ge(var_ready, count + 1)
    c.nc.scalar.activation(c.std[:, :], c.vareps[:, :], ACT.Sqrt).then_inc(std_ready, 1)


def setup(nc, c, a):
    with ExitStack() as ctx:
        s = sems(ctx, nc, "set", "weights x zeroed swapped spread spread2")
        block = ctx.enter_context(nc.Block())

        @block.sync
        def _(sp):
            for b in range(B):
                sp.dma_start(cols(c.X, b * S, S).rearrange("p (t d) -> p t d", t=QT),
                             a["x"][b].rearrange("(t p) d -> p t d", p=P)).then_inc(s.x, 16)
            loads = [
                (c.wqkv[:, :], a["w_qkv"]), (c.wproj[:, :], a["w_proj"]), (c.wq[:, :], a["w_q"]),
                (c.wk[:, :], a["w_k"]), (c.wv[:, :], a["w_v"]), (c.wo[:, :], a["w_o"]),
                (c.gate_w[:, :], a["gate_w"]), (c.cos[:, :], a["cos"]), (c.sin[:, :], a["sin"]),
                (c.w1[:, :].rearrange("p (e n) -> p e n", e=E), a["w1"].rearrange("e p n -> p e n")),
                (c.w2[:, :].rearrange("p (g n) -> p g n", g=E * HT), a["w2"].rearrange("e (k p) n -> p (e k) n", p=P)),
                (c.ln[:, 0:1], a["ln1_w"].rearrange("(p o) -> p o", o=1)),
                (c.ln[:, 1:2], a["ln1_b"].rearrange("(p o) -> p o", o=1)),
                (c.ln[:, 2:3], a["ln2_w"].rearrange("(p o) -> p o", o=1)),
                (c.ln[:, 3:4], a["ln2_b"].rearrange("(p o) -> p o", o=1)),
                (c.gate_b[:, :], a["gate_b"].rearrange("(o e) -> o e", o=1).broadcast_to((P, E))),
            ]
            for dst, src in loads:
                sp.dma_start(dst, src).then_inc(s.weights, 16)
            sp.wait_ge(s.zeroed, 1)
            for k in range(NBLK // 8):
                sp.dma_start(c.sorted_x[k * 8 * P:(k + 1) * 8 * P, :].rearrange("(p r) d -> p (r d)", p=P),
                             c.K[:, 0:8 * D].bitcast(F32)).then_inc(s.weights, 16)
            sp.wait_ge(s.x, 16 * B)
            sp.wait_ge(s.weights, 16 * (len(loads) + NBLK // 8))
            sp.sem_inc(s.spread2, 1)

        @block.gpsimd
        def _(pool):
            nc.gpsimd.memset(c.ident[:, :], 0.0)
            nc.gpsimd.memset(c.upper[:, :], 1.0)
            nc.gpsimd.memset(c.ones[:, :], 1.0).then_inc(s.spread, 1)
            pool.wait_ge(s.spread, 1)
            nc.gpsimd.affine_select(out=c.ident[:, :], in_=c.ident[:, :], compare_op=ALU.not_equal, fill=1.0,
                                    base=0, pattern=[[-1, P]], channel_multiplier=1)
            nc.gpsimd.affine_select(out=c.upper[:, :], in_=c.upper[:, :], compare_op=ALU.is_gt, fill=0.0,
                                    base=0, pattern=[[1, P]], channel_multiplier=-1)
            nc.gpsimd.iota(c.blocks_i[:, :], pattern=[[1, NBLK]], base=0, channel_multiplier=0)
            nc.gpsimd.iota(c.thresh_i[:, :], pattern=[[P, NT]], base=0, channel_multiplier=0)
            nc.gpsimd.iota(c.down_i[:, :], pattern=[[-1, E]], base=E, channel_multiplier=0).then_inc(s.spread, 1)

        @block.vector
        def _(dve):
            nc.vector.memset(c.K[:, :].bitcast(F32), 0.0).then_inc(s.zeroed, 1)
            nc.vector.memset(c.Q[:, :].bitcast(F32), 0.0)
            nc.vector.memset(c.zero_rows[:, :], 0.0)
            nc.vector.memset(c.reset[:, :], 1.0).then_inc(s.swapped, 1)
            nc.vector.memset(c.vstage[:, :], 1.0)
            nc.vector.memset(c.bank[6], 0.0)
            dve.wait_ge(s.swapped, 1)
            nc.vector.memset(c.reset[:, :].rearrange("p (e t) -> p e t", e=E)[:, :, 0:1], 0.0)
            dve.wait_ge(s.spread, 2)
            nc.vector.tensor_copy(c.blocks[:, :], c.blocks_i[:, :])
            nc.vector.tensor_copy(c.thresh[:, :], c.thresh_i[:, :])
            nc.vector.tensor_copy(c.down[:, :], c.down_i[:, :])
            dve.wait_ge(s.spread2, 1)
            nc.vector.memset(c.K[MROW:MROW + 2, :].bitcast(F32), -1.0)
            for w, sw in ((c.wq, c.wq_sw), (c.wk, c.wk_sw)):
                wv = w[:, :].rearrange("p (h t c) -> p h t c", t=2, c=HD // 2)
                sv = sw[:, :].rearrange("p (h t c) -> p h t c", t=2, c=HD // 2)
                for t in range(2):
                    ins = nc.vector.tensor_copy(sv[:, :, t, :], wv[:, :, 1 - t, :])
            ins.then_inc(s.swapped, 1)


def project(nc, c, stage, ffn):
    rows_k = P if ffn else KV * HD
    norms = 2 if ffn else 1
    with ExitStack() as ctx:
        s = sems(ctx, nc, f"p{stage}", "ln held var std transposed zT qk_ready v_ready "
                 "hi lo qkraw v_staged stored:2 rot v_stored")
        block = ctx.enter_context(nc.Block())
        w = c.work
        n_sb, zT = w[:, 0:512], w[:, 512:1024]
        hi = [w[:, 1024:1536], w[:, 1536:2048]]
        lo = [w[:, 2048:2560], w[:, 2560:3072]]
        rot = [w[:, 3072:3584], w[:, 3584:4096]]
        rot2 = [w[:, 4096:4608], w[:, 4608:5120]]
        T, qkp, vp, swp = c.bank[0], [c.bank[1], c.bank[2]], c.bank[3], [c.bank[4], c.bank[5]]
        rows = [P, rows_k]
        if ffn:
            wts = [c.wqkv[:, 0:D], c.wqkv[:, D:2 * D]]
            wv = c.wqkv[:, 2 * D:3 * D]
        else:
            wts = [c.wq[:, :], c.wk[:, :]]
            wv = c.wv[:, :]
        wsw = [c.wq_sw[:, :], c.wk_sw[:, :]]

        @block.vector
        def _(dve):
            def norm(b):
                if ffn:
                    layer_norm(dve, c, s, b * 8, lambda t: cols(c.X, b * S + t * D, D),
                               lambda t: cols(c.Y, b * S + t * D, D), s.var, s.std, 2 * b)
                    wait(dve, s.transposed, b)
                    layer_norm(dve, c, s, b * 8 + 4, lambda t: cols(c.Y, b * S + t * D, D),
                               lambda t: n_sb[:, t * D:(t + 1) * D], s.var, s.std, 2 * b + 1)
                else:
                    wait(dve, s.transposed, b)
                    layer_norm(dve, c, s, b * 4, lambda t: cols(c.X, b * S + t * D, D),
                               lambda t: n_sb[:, t * D:(t + 1) * D], s.var, s.std, b)

            def low_parts(b):
                for i in range(2):
                    r = rows[i]
                    if not ffn:
                        dve.wait_ge(s.qk_ready, 2 * b + i + 1)
                        wait(dve, s.stored[i], 16 * 2 * b)
                        nc.vector.tensor_tensor(rot[i][0:r, :], qkp[i][0:r, :], c.cos[0:r, :], ALU.mult)
                        nc.vector.tensor_tensor(rot2[i][0:r, :], swp[i][0:r, :], c.sin[0:r, :], ALU.mult).then_inc(s.rot, 1)
                        dve.wait_ge(s.rot, 4 * b + 2 * i + 1)
                        nc.vector.tensor_tensor(rot[i][0:r, :], rot[i][0:r, :], rot2[i][0:r, :], ALU.add).then_inc(s.rot, 1)
                    dve.wait_ge(s.hi, 2 * b + i + 1)
                    if ffn:
                        wait(dve, s.stored[i], 16 * 2 * b)
                    full = qkp[i] if ffn else rot[i]
                    nc.vector.tensor_tensor(lo[i][0:r, :].bitcast(F32R), full[0:r, :], hi[i][0:r, :],
                                            ALU.subtract).then_inc(s.lo, 1)

            norm(0)
            for b in (0,):
                norm(b + 1)
                low_parts(b)
            with dve.Fori(1, B - 1) as b:
                norm(b + 1)
                low_parts(b)
            low_parts(B - 1)

        @block.scalar
        def _(act):
            def roots(b):
                for k in range(norms):
                    square_root(act, c, s.var, s.std, norms * b + k)

            def evacuate(b, last=False):
                act.wait_ge(s.transposed, b + 1)
                wait(act, s.v_ready, b)
                if ffn:
                    nc.scalar.activation(zT, T[:, :], ACT.Identity, bias=c.ln[:, 1:2],
                                         scale=c.ln[:, 0:1]).then_inc(s.zT, 1)
                else:
                    nc.scalar.activation(zT, T[:, :], ACT.Copy).then_inc(s.zT, 1)
                if not last:
                    roots(b + 1)
                for i in range(2):
                    r = rows[i]
                    wait(act, s.stored[i], 16 * 2 * b)
                    if ffn:
                        act.wait_ge(s.qk_ready, 2 * b + i + 1)
                        full = qkp[i]
                    else:
                        act.wait_ge(s.rot, 4 * b + 2 * i + 2)
                        full = rot[i]
                    nc.scalar.activation(hi[i][0:r, :].bitcast(F32R), full[0:r, :], ACT.Copy).then_inc(s.hi, 1)
                act.wait_ge(s.v_ready, b + 1)
                wait(act, s.stored[0], 16 * 2 * b)
                wait(act, s.v_staged, b * QT)
                wait(act, s.v_stored, 16 * b)
                vs = c.vstage[:, :].rearrange("p (g k j e) -> p g k j e", g=G, k=QT, j=J)
                for t in range(QT):
                    src = vp[:, t * P:t * P + (D if ffn else KV * HD)]
                    if ffn:
                        src = src.rearrange("p (g j d) -> p g j d", g=G, j=J)
                    else:
                        src = src.rearrange("p (g j d) -> p g j d", g=G, j=1).broadcast_to((P, G, J, HD))
                    nc.scalar.activation(vs[:, :, t, :, 0:HD], src, ACT.Copy).then_inc(s.v_staged, 1)

            roots(0)
            evacuate(0)
            with act.Fori(1, B - 1) as b:
                evacuate(b)
            evacuate(B - 1, last=True)

        @block.tensor
        def _(pe):
            def body(b):
                pe.wait_ge(s.ln, b * 4 * norms + 4 * norms)
                wait(pe, s.zT, b)
                for t in range(QT):
                    ins = nc.tensor.transpose(T[:, t * P:(t + 1) * P], n_sb[:, t * D:(t + 1) * D], c.ident[:, :])
                ins.then_inc(s.transposed, 1)
                pe.wait_ge(s.zT, b + 1)
                wait(pe, s.lo, 2 * b)
                for i in range(2):
                    if not ffn:
                        nc.tensor.matmul(swp[i][0:rows[i], :], wsw[i], zT, start=True, stop=True)
                    nc.tensor.matmul(qkp[i][0:rows[i], :], wts[i], zT, start=True, stop=True).then_inc(s.qk_ready, 1)
                wait(pe, s.v_staged, b * QT)
                nv = D if ffn else KV * HD
                for t in range(QT):
                    ins = nc.tensor.matmul(vp[:, t * P:t * P + nv], zT[:, t * P:(t + 1) * P], wv, start=True, stop=True)
                ins.then_inc(s.v_ready, 1)

            batches(pe, body)

        @block.sync
        def _(sp):
            def body(b):
                for i in range(2):
                    sp.wait_ge(s.hi, 2 * b + i + 1)
                    sp.dma_start(c.qk_scratch[bass.ds(b * 4 + 2 * i, 1), 0:rows[i], :].rearrange("o r n -> (o r) n"),
                                 hi[i][0:rows[i], :]).then_inc(s.stored[i], 16)
                    sp.wait_ge(s.lo, 2 * b + i + 1)
                    sp.dma_start(c.qk_scratch[bass.ds(b * 4 + 2 * i + 1, 1), 0:rows[i], :].rearrange("o r n -> (o r) n"),
                                 lo[i][0:rows[i], :]).then_inc(s.stored[i], 16)
                sp.wait_ge(s.v_staged, (b + 1) * QT)
                sp.dma_start(c.v_scratch[bass.ds(b * G, G), :, :].rearrange("g p n -> p g n"),
                             c.vstage[:, :].rearrange("p (g n) -> p g n", g=G)).then_inc(s.v_stored, 16)

            batches(sp, body)
            for i in range(2):
                sp.wait_ge(s.stored[i], 32 * B)
            sp.wait_ge(s.v_stored, 16 * B)


def attend(nc, c, stage, ffn):
    with ExitStack() as ctx:
        s = sems(ctx, nc, f"t{stage}", "max_scores max_taken max_turned max_split max_rows:4 loaded:4 "
                 "scores probs pv out_copied out_turned out_normed recip")
        block = ctx.enter_context(nc.Block())
        LOADS = 10
        maxp = [c.bank[0], c.bank[1]]
        scp = [c.pair[0], c.pair[1]]
        outp, misc = c.bank[6], c.bank[7]
        prob = c.work[:, :].rearrange("p (r j n) -> p r j n", r=4, j=J)
        q4 = c.Q[:, :].rearrange("p (s j n) -> p s j n", s=4, j=J)
        k4 = c.K[:, :].rearrange("p (s j n) -> p s j n", s=4, j=J)
        v4 = c.V[:, :].rearrange("p (s k j e) -> p s k j e", s=4, k=QT, j=J)

        def where(b, g, ahead):
            b2, g2 = b + (g + ahead) // G, (g + ahead) % G
            if isinstance(b, int) and b2 >= B:
                return None
            return b2, g2, G * b2 + g2

        @block.sync
        def _(sp):
            def load(b, g, n):
                wait(sp, s.pv, 4 * (n - 3))
                done = s.loaded[g]
                for i, ring in enumerate((q4, k4)):
                    for part in range(4):
                        hl = part // 2 if i == 0 else part % 2
                        src = c.qk_scratch[bass.ds(b * 4 + 2 * i + hl, 1), :, :]
                        if ffn or i == 0:
                            src = src[:, g * J * HD:(g + 1) * J * HD, :].rearrange("o (j d) n -> (o d) j n", j=J)
                        else:
                            src = src[:, g * HD:(g + 1) * HD, :].rearrange("o (j d) n -> (o d) j n", j=1)\
                                .broadcast_to((HD, J, S))
                        sp.dma_start(ring[part * HD:(part + 1) * HD, g, :, :].bitcast(F32), src).then_inc(done, 16)
                sp.dma_start(c.Q[MROW:MROW + 2, g * SLOT:(g + 1) * SLOT].bitcast(F32), c.zero_rows[:, :]).then_inc(done, 16)
                sp.dma_start(c.V[:, g * QT * J * V1:(g + 1) * QT * J * V1],
                             c.v_scratch[bass.ds(b * G + g, 1), :, :].rearrange("o p n -> (o p) n")).then_inc(done, 16)

            def rows_of_max(b, g, n):
                sp.wait_ge(s.max_split, 2 * n + 2)
                for i in range(2):
                    sp.dma_start(c.Q[MROW + i:MROW + i + 1, g * SLOT:(g + 1) * SLOT].bitcast(F32).rearrange("o (r n) -> o r n", n=P),
                                 c.maxT[:, (2 * (g % 2) + i) * P:(2 * (g % 2) + i + 1) * P].bitcast(F32))\
                        .then_inc(s.max_rows[g], 16)

            for n in range(3):
                load(0, n, n)
            rows_of_max(0, 0, 0)

            def body(b):
                for g in range(G):
                    nxt = where(b, g, 1)
                    if nxt:
                        rows_of_max(*nxt)
                    ahead = where(b, g, 3)
                    if ahead:
                        load(*ahead)

            batches(sp, body)
            for g in range(G):
                sp.wait_ge(s.max_rows[g], 32 * B)

        @block.tensor
        def _(pe):
            def max_scores(b, g, n, j, qt):
                u = 16 * n + 4 * j + qt
                wait(pe, s.max_taken, u - 1)
                nc.tensor.matmul(maxp[qt % 2][:, :], q4[:, g, j, qt * P:(qt + 1) * P], k4[:, g, j, :],
                                 start=True, stop=True).then_inc(s.max_scores, 1)

            def turn_max(b, g, n):
                wait(pe, s.max_taken, 16 * (n + 1))
                wait(pe, s.max_split, 2 * n)
                wait(pe, s.out_normed, n - 2)
                nc.tensor.transpose(misc[0:16, 0:P], c.maxima[:, 16 * (g % 2):16 * (g % 2) + 16],
                                    c.ident[:, :]).then_inc(s.max_turned, 1)

            def scores(b, g, n, kt, half):
                w = 2 * (4 * n + kt) + half
                wait(pe, s.probs, w - 1)
                for i in range(2):
                    j = 2 * half + i
                    ins = nc.tensor.matmul(scp[half][:, i * S:(i + 1) * S], k4[:, g, j, kt * P:(kt + 1) * P],
                                           q4[:, g, j, :], start=True, stop=True)
                ins.then_inc(s.scores, 1)

            def weigh(b, g, n, kt):
                pe.wait_ge(s.probs, 2 * (4 * n + kt) + 2)
                if kt == 0:
                    wait(pe, s.out_copied, n)
                for j in range(J):
                    ins = nc.tensor.matmul(outp[32 * j:32 * j + V1, :], v4[:, g, kt, j, :], prob[:, kt, j, :],
                                           start=(kt == 0), stop=(kt == QT - 1))
                ins.then_inc(s.pv, 1)

            def turn_out(b, g, n):
                pe.wait_ge(s.out_copied, n + 1)
                wait(pe, s.out_normed, n)
                wait(pe, s.max_split, 2 * min(n + 3, NG) if isinstance(n, int) else 2 * n + 6)
                for t in range(QT):
                    ins = nc.tensor.transpose(misc[:, t * P:(t + 1) * P], c.outT[:, t * P:(t + 1) * P], c.ident[:, :])
                ins.then_inc(s.out_turned, 1)

            for n in range(2):
                pe.wait_ge(s.loaded[n], 16 * LOADS)
                for j in range(J):
                    for qt in range(QT):
                        max_scores(0, n, n, j, qt)
                if n == 0:
                    turn_max(0, 0, 0)

            def step(b, g, kt, before):
                n = G * b + g
                ahead = where(b, g, 2)
                if kt == 0:
                    pe.wait_ge(s.max_rows[g], 32 * (b + 1))
                    if ahead:
                        pe.wait_ge(s.loaded[ahead[1]], 16 * LOADS * (ahead[0] + 1))
                    nxt = where(b, g, 1)
                scores(b, g, n, kt, 0)
                if ahead:
                    max_scores(*ahead, kt, 0)
                    max_scores(*ahead, kt, 1)
                scores(b, g, n, kt, 1)
                if ahead:
                    max_scores(*ahead, kt, 2)
                    max_scores(*ahead, kt, 3)
                if kt == 0 and nxt:
                    turn_max(*nxt)
                if before:
                    weigh(*before)
                if kt == 2 and not (isinstance(b, int) and n == 0):
                    turn_out(b, g, n - 1)

            def body(b):
                for g in range(G):
                    for kt in range(QT):
                        if kt:
                            before = (b, g, G * b + g, kt - 1)
                        elif g:
                            before = (b, g - 1, G * b + g - 1, QT - 1)
                        elif isinstance(b, int) and b == 0:
                            before = None
                        else:
                            before = (b - 1, G - 1, G * b - 1, QT - 1)
                        step(b, g, kt, before)

            batches(pe, body)
            weigh(B - 1, G - 1, NG - 1, QT - 1)
            turn_out(B - 1, G - 1, NG - 1)

        @block.scalar
        def _(act):
            def copy_out(n):
                act.wait_ge(s.pv, 4 * n + 4)
                wait(act, s.out_turned, n)
                nc.scalar.activation(c.outT[:, :], outp[:, :], ACT.Copy).then_inc(s.out_copied, 1)

            def body(b):
                for g in range(G):
                    n = G * b + g
                    for kt in range(QT):
                        if kt == 1 and not (isinstance(b, int) and n == 0):
                            copy_out(n - 1)
                        for half in range(2):
                            t = 4 * n + kt
                            act.wait_ge(s.scores, 2 * t + half + 1)
                            wait(act, s.pv, t - 3)
                            nc.scalar.activation(prob[:, kt, 2 * half:2 * half + 2, :], scp[half][:, :]
                                                 .rearrange("p (j n) -> p j n", j=2), ACT.Exp,
                                                 scale=SCALE).then_inc(s.probs, 1)

            batches(act, body)
            copy_out(NG - 1)

        @block.vector
        def _(dve):
            def take_max(b, g, n, j, qt):
                u = 16 * n + 4 * j + qt
                dve.wait_ge(s.max_scores, u + 1)
                if j == 0 and qt == 0:
                    wait(dve, s.max_turned, n - 1)
                k = 16 * (g % 2) + 4 * j + qt
                nc.vector.tensor_reduce(c.maxima[:, k:k + 1], maxp[qt % 2][:, :], AX.X, ALU.max).then_inc(s.max_taken, 1)

            def split_max(b, g, n):
                dve.wait_ge(s.max_turned, n + 1)
                if isinstance(n, int):
                    if n >= 2:
                        dve.wait_ge(s.max_rows[(n - 2) % 4], 32 * ((n - 2) // 4 + 1))
                elif g >= 2:
                    dve.wait_ge(s.max_rows[g - 2], 32 * (b + 1))
                else:
                    dve.wait_ge(s.max_rows[g + 2], 32 * b)
                hi = c.maxT[:, 2 * (g % 2) * P:(2 * (g % 2) + 1) * P]
                lo = c.maxT[:, (2 * (g % 2) + 1) * P:(2 * (g % 2) + 2) * P]
                nc.vector.tensor_copy(hi, misc[0:16, 0:P]).then_inc(s.max_split, 1)
                dve.wait_ge(s.max_split, 2 * n + 1)
                nc.vector.tensor_tensor(lo, misc[0:16, 0:P], hi.bitcast(F32), ALU.subtract).then_inc(s.max_split, 1)

            def normalise(b, g, n):
                dve.wait_ge(s.out_turned, n + 1)
                turned = misc[:, :].rearrange("p (t j r) -> p t j r", t=QT, j=J)
                rec = c.recip[:, :].rearrange("p (t j) -> p t j", t=QT)
                nc.vector.reciprocal(rec, turned[:, :, :, HD]).then_inc(s.recip, 1)
                dve.wait_ge(s.recip, n + 1)
                dst = cols(c.N, b * S, S).rearrange("p (t g j d) -> p t g j d", t=QT, g=G, j=J)[:, :, g, :, :]
                nc.vector.tensor_tensor(dst, turned[:, :, :, 0:HD],
                                        rec.rearrange("p t (j o) -> p t j o", o=1).broadcast_to((P, QT, J, HD)),
                                        ALU.mult).then_inc(s.out_normed, 1)

            for n in range(2):
                for j in range(J):
                    for qt in range(QT):
                        take_max(0, n, n, j, qt)
                if n == 0:
                    split_max(0, 0, 0)

            def body(b):
                for g in range(G):
                    n = G * b + g
                    ahead, nxt = where(b, g, 2), where(b, g, 1)
                    for kt in range(QT):
                        if ahead:
                            take_max(*ahead, kt, 0)
                            take_max(*ahead, kt, 1)
                        if kt == 1 and nxt:
                            split_max(*nxt)
                        if kt == 3 and not (isinstance(b, int) and n == 0):
                            if g:
                                normalise(b, g - 1, n - 1)
                            else:
                                normalise(b - 1, G - 1, n - 1)
                        if ahead:
                            take_max(*ahead, kt, 2)
                            take_max(*ahead, kt, 3)

            batches(dve, body)
            normalise(B - 1, G - 1, NG - 1)


def finish_attention(nc, c, stage, ffn):
    with ExitStack() as ctx:
        s = sems(ctx, nc, f"o{stage}", "staged turned aT proj added ln held var std nT uT logit logged kept")
        block = ctx.enter_context(nc.Block())
        w = c.work
        a_sb, aT, n_sb, uT = w[:, 0:512], w[:, 512:1024], w[:, 1024:1536], w[:, 1536:2048]
        T, pp, T2, lp = c.bank[0], c.bank[1], c.bank[2], c.bank[3]
        weight = c.wproj if ffn else c.wo
        res = c.Y if ffn else c.X

        @block.gpsimd
        def _(pool):
            def keep(b):
                pool.wait_ge(s.ln, 4 * b + 4)
                nc.gpsimd.tensor_copy(cols(c.N, b * S, S), n_sb).then_inc(s.kept, 1)

            def stage_in(b):
                wait(pool, s.turned, b)
                nc.gpsimd.tensor_copy(a_sb, cols(c.N, b * S, S)).then_inc(s.staged, 1)

            stage_in(0)

            def body(b):
                stage_in(b + 1)
                if ffn:
                    keep(b)

            body(0)
            with pool.Fori(1, B - 1) as b:
                body(b)
            if ffn:
                keep(B - 1)

        @block.tensor
        def _(pe):
            def body(b):
                pe.wait_ge(s.staged, b + 1)
                wait(pe, s.aT, b)
                for t in range(QT):
                    ins = nc.tensor.transpose(T[:, t * P:(t + 1) * P], a_sb[:, t * P:(t + 1) * P], c.ident[:, :])
                ins.then_inc(s.turned, 1)
                pe.wait_ge(s.aT, b + 1)
                wait(pe, s.added, b)
                for t in range(QT):
                    ins = nc.tensor.matmul(pp[:, t * P:(t + 1) * P], aT[:, t * P:(t + 1) * P], weight[:, :],
                                           start=True, stop=True)
                ins.then_inc(s.proj, 1)
                if ffn:
                    pe.wait_ge(s.ln, 4 * b + 4)
                    wait(pe, s.uT, b)
                    for t in range(QT):
                        ins = nc.tensor.transpose(T2[:, t * P:(t + 1) * P], n_sb[:, t * P:(t + 1) * P], c.ident[:, :])
                    ins.then_inc(s.nT, 1)
                    pe.wait_ge(s.uT, b + 1)
                    wait(pe, s.logged, b)
                    for t in range(QT):
                        ins = nc.tensor.matmul(lp[:, t * E:(t + 1) * E], uT[:, t * P:(t + 1) * P], c.gate_w[:, :],
                                               start=True, stop=True)
                    ins.then_inc(s.logit, 1)

            batches(pe, body)

        @block.scalar
        def _(act):
            def body(b):
                act.wait_ge(s.turned, b + 1)
                wait(act, s.proj, b)
                nc.scalar.activation(aT, T[:, :], ACT.Copy).then_inc(s.aT, 1)
                if ffn:
                    square_root(act, c, s.var, s.std, b)
                    act.wait_ge(s.nT, b + 1)
                    wait(act, s.logit, b)
                    nc.scalar.activation(uT, T2[:, :], ACT.Identity, bias=c.ln[:, 3:4],
                                         scale=c.ln[:, 2:3]).then_inc(s.uT, 1)

            batches(act, body)

        @block.vector
        def _(dve):
            def body(b):
                dve.wait_ge(s.proj, b + 1)
                nc.vector.tensor_tensor(cols(res, b * S, S), pp[:, :], cols(res, b * S, S), ALU.add).then_inc(s.added, 1)
                if ffn:
                    dve.wait_ge(s.added, b + 1)
                    wait(dve, s.nT, b)
                    wait(dve, s.kept, b)
                    layer_norm(dve, c, s, 4 * b, lambda t: cols(c.Y, b * S + t * D, D),
                               lambda t: n_sb[:, t * D:(t + 1) * D], s.var, s.std, b)
                    dve.wait_ge(s.logit, b + 1)
                    nc.vector.tensor_tensor(
                        cols(c.logits, b * QT * E, QT * E).rearrange("p (t e) -> p t e", t=QT),
                        lp[:, 0:QT * E].rearrange("p (t e) -> p t e", t=QT),
                        c.gate_b[:, :].rearrange("p (o e) -> p o e", o=1).broadcast_to((P, QT, E)),
                        ALU.add).then_inc(s.logged, 1)

            batches(dve, body)


def route(nc, c, stage):
    with ExitStack() as ctx:
        s = sems(ctx, nc, f"r{stage}", "chain onehot counted positions scattered")
        block = ctx.enter_context(nc.Block())
        TE = NT * E
        w = c.work
        mask, val, onehot = w[:, 0:TE], w[:, TE:2 * TE], w[:, 2 * TE:3 * TE]
        tot, inc, off = w[:, 3 * TE:4 * TE], w[:, 4 * TE:5 * TE], w[:, 5 * TE:6 * TE]
        big = w[:, 2048:2048 + NBLK * E]
        small = w[:, 3072:3072 + 256]
        best, top = small[:, 0:NT], small[:, NT:2 * NT]
        nblk, ends, base = small[:, 64:72], small[:, 72:80], small[:, 80:88]
        blk, posf, ones8 = small[:, 96:96 + NBLK], small[:, 160:192], small[:, 200:208]
        rank_ps, tot_ps = c.bank[0], c.bank[1]

        def te(x):
            return x.rearrange("p (t e) -> p t e", e=E)

        def et(x):
            return x.rearrange("p (e t) -> p e t", e=E)

        def inner(x, n):
            return x.rearrange("p (a o) -> p a o", o=1).broadcast_to((P, x.shape[1], n))

        def outer(x, n):
            return x.rearrange("p (o a) -> p o a", o=1).broadcast_to((P, n, x.shape[1]))

        @block.vector
        def _(dve):
            links = [0]

            def link(ins):
                links[0] += 1
                ins.then_inc(s.chain, 1)
                dve.wait_ge(s.chain, links[0])

            lg = te(c.logits[:, :])
            link(nc.vector.tensor_reduce(top, lg, AX.X, ALU.max))
            link(nc.vector.tensor_tensor(te(mask), lg, inner(top, E), ALU.is_equal))
            link(nc.vector.tensor_tensor(te(val), te(mask), outer(c.down[:, :], NT), ALU.mult))
            link(nc.vector.tensor_reduce(best, te(val), AX.X, ALU.max))
            nc.vector.memset(ones8, 1.0)
            nc.vector.tensor_tensor(te(onehot), te(val), inner(best, E), ALU.is_equal).then_inc(s.onehot, 1)
            dve.wait_ge(s.counted, 2)
            link(nc.vector.tensor_copy(et(tot), te(tot_ps[:, 0:TE]).rearrange("p t e -> p e t")))
            link(nc.vector.tensor_tensor_scan(inc, c.reset[:, :], tot, 0.0, ALU.mult, ALU.add))
            link(nc.vector.tensor_tensor(off, inc, tot, ALU.subtract))
            cnt = et(inc)[:, :, NT - 1]
            link(nc.vector.tensor_tensor(et(mask), cnt.rearrange("p (e o) -> p e o", o=1).broadcast_to((P, E, NT)),
                                         outer(c.thresh[:, :], E), ALU.is_gt))
            link(nc.vector.tensor_reduce(nblk, et(mask), AX.X, ALU.add))
            link(nc.vector.tensor_tensor_scan(ends, ones8, nblk, 0.0, ALU.mult, ALU.add))
            link(nc.vector.tensor_tensor(base, ends, nblk, ALU.subtract))
            link(nc.vector.tensor_scalar(base, base, float(P), None, ALU.mult))
            link(nc.vector.tensor_tensor(et(off), et(off), inner(base, NT), ALU.add))
            link(nc.vector.tensor_tensor(te(val), te(rank_ps[:, 0:TE]), et(off).rearrange("p e t -> p t e"), ALU.add))
            link(nc.vector.tensor_tensor(te(val), te(val), te(onehot), ALU.mult))
            link(nc.vector.tensor_reduce(posf, te(val), AX.X, ALU.add))
            nc.vector.tensor_copy(c.pos[:, :], posf).then_inc(s.positions, 1)
            bg = big.rearrange("p (b e) -> p b e", e=E)
            link(nc.vector.tensor_tensor(bg, inner(c.blocks[:, :], E), outer(ends, NBLK), ALU.is_ge))
            link(nc.vector.tensor_reduce(blk, bg, AX.X, ALU.add))
            link(nc.vector.tensor_scalar(blk, blk, float(E - 1), float(HID), ALU.min, ALU.mult))
            link(nc.vector.tensor_copy(c.expert_at[:, :], blk[0:1, :]))

        @block.tensor
        def _(pe):
            pe.wait_ge(s.onehot, 1)
            nc.tensor.matmul(rank_ps[:, 0:TE], c.upper[:, :], onehot, start=True, stop=True).then_inc(s.counted, 1)
            nc.tensor.matmul(tot_ps[:, 0:TE], c.ones[:, :], onehot, start=True, stop=True).then_inc(s.counted, 1)

        @block.gpsimd
        def _(pool):
            pool.wait_ge(s.positions, 1)
            for t in range(NT):
                nc.gpsimd.indirect_dma_start(
                    c.sorted_x[:, :], bass.IndirectOffsetOnAxis(ap=c.pos[:, t:t + 1], axis=0),
                    c.N[:, t * D:(t + 1) * D], None).then_inc(s.scattered, 16)
            pool.wait_ge(s.scattered, 16 * NT)


def experts(nc, c, stage):
    with ExitStack() as ctx:
        s = sems(ctx, nc, f"e{stage}", "loaded:2 turned uT hidden gelu hidden_turned hT out out_copied stored:2")
        block = ctx.enter_context(nc.Block())
        w = c.work
        x_sb = [w[:, 0:128], w[:, 128:256]]
        uT = [w[:, 256:384], w[:, 384:512]]
        h_sb = [w[:, 512:1024], w[:, 1024:1536]]
        hT = [w[:, 1536:2048], w[:, 2048:2560]]
        y_sb = [w[:, 2560:2688], w[:, 2688:2816]]
        Tp, hp, hTp, yp = [c.bank[0], c.bank[1]], [c.bank[2], c.bank[3]], [c.bank[4], c.bank[5]], [c.bank[6], c.bank[7]]

        def blocks(eng, step):
            step(0, 0, 0)
            step(1, 1, 0)
            with eng.Fori(1, NBLK // 2 - 1) as k:
                step(2 * k, 0, k)
                step(2 * k + 1, 1, k)
            step(NBLK - 2, 0, NBLK // 2 - 1)
            step(NBLK - 1, 1, NBLK // 2 - 1)

        def past_end(i):
            return isinstance(i, int) and i >= NBLK

        @block.sync
        def _(sp):
            def load(i, par, k):
                wait(sp, s.turned, i - 1)
                sp.dma_start(x_sb[par], c.sorted_x[bass.ds(i * P, P), :]).then_inc(s.loaded[par], 16)

            def step(i, par, k):
                if not past_end(i + 1):
                    load(i + 1, 1 - par, k + par)
                sp.wait_ge(s.out_copied, i + 1)
                sp.dma_start(c.sorted_y[bass.ds(i * P, P), :], y_sb[par]).then_inc(s.stored[par], 16)

            load(0, 0, 0)
            blocks(sp, step)
            for par in range(2):
                sp.wait_ge(s.stored[par], 16 * NBLK // 2)

        @block.tensor
        def _(pe):
            def turn(i, par, k):
                pe.wait_ge(s.loaded[par], 16 * (k + 1))
                wait(pe, s.uT, i - 1)
                nc.tensor.transpose(Tp[par][:, 0:P], x_sb[par], c.ident[:, :]).then_inc(s.turned, 1)

            def hidden(i, par, at):
                pe.wait_ge(s.uT, i + 1)
                wait(pe, s.gelu, i - 1)
                nc.tensor.matmul(hp[par][:, :], uT[par], cols(c.w1, at, HID), start=True, stop=True).then_inc(s.hidden, 1)

            def turn_hidden(i, par):
                pe.wait_ge(s.gelu, i + 1)
                wait(pe, s.hT, i - 1)
                for t in range(HT):
                    ins = nc.tensor.transpose(hTp[par][:, t * P:(t + 1) * P], h_sb[par][:, t * P:(t + 1) * P], c.ident[:, :])
                ins.then_inc(s.hidden_turned, 1)

            def output(i, par, at):
                pe.wait_ge(s.hT, i + 1)
                wait(pe, s.out_copied, i - 1)
                for t in range(HT):
                    ins = nc.tensor.matmul(yp[par][:, 0:D], hT[par][:, t * P:(t + 1) * P], cols(c.w2, at + t * D, D),
                                           start=(t == 0), stop=(t == HT - 1))
                ins.then_inc(s.out, 1)

            def expert(i):
                return pe.value_load(c.expert_at[0:1, bass.ds(i, 1)], min_val=0, max_val=(E - 1) * HID)

            def step(i, par, k):
                if not past_end(i + 1):
                    turn(i + 1, 1 - par, k + par)
                turn_hidden(i, par)
                if not past_end(i + 1):
                    hidden(i + 1, 1 - par, expert(i + 1))
                output(i, par, expert(i))

            turn(0, 0, 0)
            hidden(0, 0, expert(0))
            blocks(pe, step)

        @block.scalar
        def _(act):
            def affine(i, par):
                act.wait_ge(s.turned, i + 1)
                wait(act, s.hidden, i - 1)
                nc.scalar.activation(uT[par], Tp[par][:, 0:P], ACT.Identity, bias=c.ln[:, 3:4],
                                     scale=c.ln[:, 2:3]).then_inc(s.uT, 1)

            def step(i, par, k):
                if not past_end(i + 1):
                    affine(i + 1, 1 - par)
                act.wait_ge(s.hidden, i + 1)
                wait(act, s.hidden_turned, i - 1)
                nc.scalar.activation(h_sb[par], hp[par][:, :], ACT.Gelu_apprx_tanh).then_inc(s.gelu, 1)

            affine(0, 0)
            blocks(act, step)

        @block.vector
        def _(dve):
            def step(i, par, k):
                dve.wait_ge(s.hidden_turned, i + 1)
                wait(dve, s.out, i - 1)
                nc.vector.tensor_copy(hT[par], hTp[par][:, :]).then_inc(s.hT, 1)
                dve.wait_ge(s.out, i + 1)
                wait(dve, s.stored[par], 16 * k)
                nc.vector.tensor_copy(y_sb[par], yp[par][:, 0:D]).then_inc(s.out_copied, 1)

            blocks(dve, step)


def combine(nc, c, stage, out):
    with ExitStack() as ctx:
        s = sems(ctx, nc, f"c{stage}", f"gathered:{B} summed done stored")
        block = ctx.enter_context(nc.Block())

        @block.gpsimd
        def _(pool):
            for t in range(NT):
                nc.gpsimd.indirect_dma_start(
                    c.N[:, t * D:(t + 1) * D], None,
                    c.sorted_y[:, :], bass.IndirectOffsetOnAxis(ap=c.pos[:, t:t + 1], axis=0))\
                    .then_inc(s.gathered[t // QT], 16)

        @block.vector
        def _(dve):
            for b in range(B):
                dve.wait_ge(s.gathered[b], 16 * QT)
                n, y, x = (cols(v, b * S, S) for v in (c.N, c.Y, c.X))
                nc.vector.tensor_tensor(n, n, y, ALU.add).then_inc(s.summed, 1)
                dve.wait_ge(s.summed, b + 1)
                nc.vector.scalar_tensor_tensor(out=x, in0=n, scalar=0.5, in1=x, op0=ALU.mult, op1=ALU.add)\
                    .then_inc(s.done, 1)

        if out is not None:
            @block.sync
            def _(sp):
                for b in range(B):
                    sp.wait_ge(s.done, b + 1)
                    sp.dma_start(out[b].rearrange("(t p) d -> p t d", p=P),
                                 cols(c.X, b * S, S).rearrange("p (t d) -> p t d", t=QT)).then_inc(s.stored, 16)
                sp.wait_ge(s.stored, 16 * B)


def build(nc, a, out):
    with ExitStack() as ctx:
        def sb(name, shape, dt=F32):
            return ctx.enter_context(nc.sbuf_tensor(name, shape, dt))

        c = Core()
        c.nc = nc
        c.X, c.Y, c.N = (sb(n, [P, B * S]) for n in ("X", "Y", "N"))
        c.Q, c.K = sb("Q", [P, 4 * SLOT], F32R), sb("K", [P, 4 * SLOT], F32R)
        c.V = sb("V", [P, 4 * QT * J * V1])
        c.work = sb("work", [P, 4 * SLOT])
        c.outT = sb("outT", [P, S])
        c.w1, c.w2 = sb("w1", [P, E * HID]), sb("w2", [P, E * HID])
        c.wqkv, c.wproj, c.wq, c.wo = sb("wqkv", [P, 3 * D]), sb("wproj", [P, D]), sb("wq", [P, D]), sb("wo", [P, D])
        c.wq_sw, c.wk, c.wk_sw, c.wv = sb("wq_sw", [P, D]), sb("wk", [P, KV * HD]), sb("wk_sw", [P, KV * HD]), sb("wv", [P, KV * HD])
        c.gate_w, c.gate_b, c.ln = sb("gate_w_sb", [P, E]), sb("gate_b_sb", [P, E]), sb("ln", [P, 4])
        c.cos, c.sin = sb("cos_sb", [P, S]), sb("sin_sb", [P, S])
        c.vstage = sb("vstage", [P, G * QT * J * V1])
        c.stats, c.moments = sb("stats", [P, QT, 6]), sb("moments", [P, QT, 2])
        c.vareps, c.std, c.rstd = sb("vareps", [P, QT]), sb("std", [P, QT]), sb("rstd", [P, QT])
        c.ident, c.upper, c.ones = sb("ident", [P, P]), sb("upper", [P, P]), sb("ones", [P, P])
        c.maxima = sb("maxima", [P, 32])
        c.maxT = sb("maxT", [16, 4 * P], F32R)
        c.zero_rows = sb("zero_rows", [2, SLOT])
        c.recip = sb("recip", [P, QT * J])
        c.logits, c.reset = sb("logits", [P, NT * E]), sb("reset", [P, E * NT])
        c.pos, c.expert_at = sb("pos", [P, NT], U32), sb("expert_at", [1, NBLK], U32)
        c.blocks_i, c.thresh_i, c.down_i = sb("blocks_i", [P, NBLK], U32), sb("thresh_i", [P, NT], U32), sb("down_i", [P, E], U32)
        c.blocks, c.thresh, c.down = sb("blocks", [P, NBLK]), sb("thresh", [P, NT]), sb("down", [P, E])
        banks = ctx.enter_context(nc.psum_tensor("banks", [P, 8 * 512], F32))
        c.bank = [banks[:, i * 512:(i + 1) * 512] for i in range(8)]
        c.pair = [banks[:, 1024:2048], banks[:, 2048:3072]]
        c.qk_scratch = nc.dram_tensor("qk_scratch", [B * 4, P, S], F32).ap()
        c.v_scratch = nc.dram_tensor("v_scratch", [B * G, P, QT * J * V1], F32).ap()
        c.sorted_x = nc.dram_tensor("sorted_x", [NBLK * P, D], F32).ap()
        c.sorted_y = nc.dram_tensor("sorted_y", [NBLK * P, D], F32).ap()

        setup(nc, c, a)
        for stage, ffn in enumerate((True, False, True)):
            project(nc, c, stage, ffn)
            attend(nc, c, stage, ffn)
            finish_attention(nc, c, stage, ffn)
            if ffn:
                route(nc, c, stage)
                experts(nc, c, stage)
                combine(nc, c, stage, out if stage == 2 else None)


def rope_tables():
    half = HD // 2
    inv = (np.float32(1.0) / np.float32(10000.0) ** (np.arange(half, dtype=np.float32) * np.float32(2.0) / np.float32(HD)))
    freq = np.arange(S, dtype=np.float32)[None, :] * inv.astype(np.float32)[:, None]
    cos, sin = np.cos(freq).astype(np.float32), np.sin(freq).astype(np.float32)
    return (np.tile(np.concatenate([cos, cos]), (H, 1)), np.tile(np.concatenate([-sin, sin]), (H, 1)))


def kernel(**inputs):
    import concourse.bacc as bacc
    from concourse.bass_utils import run_bass_kernel_spmd

    names = {
        "x": "L0_attn_x", "w_q": "L0_attn_w_q", "w_k": "L0_attn_w_k", "w_v": "L0_attn_w_v", "w_o": "L0_attn_w_o",
        "ln1_w": "L0_ffn_ln1_w", "ln1_b": "L0_ffn_ln1_b", "w_qkv": "L0_ffn_w_qkv", "w_proj": "L0_ffn_w_proj",
        "ln2_w": "L0_ffn_ln2_w", "ln2_b": "L0_ffn_ln2_b", "gate_w": "L0_ffn_gate_w", "gate_b": "L0_ffn_gate_b",
        "w1": "L0_ffn_w1", "w2": "L0_ffn_w2",
    }
    data = {k: np.ascontiguousarray(inputs[v]) for k, v in names.items()}
    data["cos"], data["sin"] = rope_tables()
    nc = bacc.Bacc("TRN2", target_bir_lowering=False, num_devices=1)
    arrays, args = {}, {}
    for k, v in data.items():
        arrays[f"in_{k}"] = v
        args[k] = nc.dram_tensor(f"in_{k}", v.shape, mybir.dt.from_np(v.dtype), kind="ExternalInput").ap()
    out = nc.dram_tensor("out_x", (B, S, D), F32, kind="ExternalOutput").ap()
    build(nc, args, out)
    r = run_bass_kernel_spmd(nc, [arrays], core_ids=[0])
    return r.results[0]["out_x"]
```

```python
from collections import namedtuple
from contextlib import ExitStack

import numpy as np
import concourse.bass as bass
from concourse import mybir

F32 = mybir.dt.float32
F32R = mybir.dt.float32r
U32 = mybir.dt.uint32
ALU = mybir.AluOpType
ACT = mybir.ActivationFunctionType
AX = mybir.AxisListType

P = 128
B, S, D = 8, 512, 128
H, HD = 16, 8
QT = S // P
NT = B * QT
G, J = 4, 4
NG = B * G
KV = 4
E, HID = 8, 512
HT = HID // P
V1 = HD + 1
NBLK = NT + E
EPS = 1e-5
SCALE = float(1.0 / np.sqrt(HD))
MROW = 32
SLOT = J * S


def wait(eng, sem, value):
    if isinstance(value, int) and value <= 0:
        return
    eng.wait_ge(sem, value)


def batches(eng, body):
    body(0)
    with eng.Fori(1, B - 1) as b:
        body(b)
    body(B - 1)


def cols(tile, start, n):
    return tile[:, bass.ds(start, n)]


class Core:
    pass


def sems(ctx, nc, tag, names):
    handles, fields, values = [], [], []
    for entry in names.split():
        name, _, n = entry.partition(":")
        new = [nc.alloc_semaphore(name=f"{tag}_{name}{i}") for i in range(int(n or 1))]
        handles += new
        fields.append(name)
        values.append(new if n else new[0])

    def clear():
        nc.clear_and_free_semaphores(handles)
        nc.all_engine_barrier()

    ctx.callback(clear)
    return namedtuple("Sems", fields)(*values)




def layer_norm(dve, c, s, value, src, dst, var_ready, std_ready, count):
    nc = c.nc
    dve.sem_inc(s.held, 1)
    for t in range(QT):
        ins = nc.vector.bn_stats(c.stats[:, t, :], src(t))
    ins.then_inc(s.ln, 1)
    dve.wait_ge(s.ln, value + 1)
    dve.sem_inc(s.held, 1)
    for t in range(QT):
        ins = nc.vector.bn_aggr(c.moments[:, t, :], c.stats[:, t, :])
    ins.then_inc(s.ln, 1)
    dve.wait_ge(s.ln, value + 2)
    nc.vector.tensor_scalar(c.vareps[:, :], c.moments[:, :, 1], EPS, None, ALU.add).then_inc(var_ready, 1)
    dve.wait_ge(std_ready, count + 1)
    nc.vector.reciprocal(c.rstd[:, :], c.std[:, :]).then_inc(s.ln, 1)
    dve.wait_ge(s.ln, value + 3)
    for t in range(QT):
        ins = nc.vector.tensor_scalar(dst(t), src(t), c.moments[:, t, 0:1], c.rstd[:, t:t + 1],
                                      ALU.subtract, ALU.mult)
    ins.then_inc(s.ln, 1)
    dve.wait_ge(s.ln, value + 4)


def square_root(act, c, var_ready, std_ready, count):
    act.wait_ge(var_ready, count + 1)
    c.nc.scalar.activation(c.std[:, :], c.vareps[:, :], ACT.Sqrt).then_inc(std_ready, 1)


def setup(nc, c, a):
    with ExitStack() as ctx:
        s = sems(ctx, nc, "set", "weights x zeroed swapped spread")
        block = ctx.enter_context(nc.Block())

        @block.sync
        def _(sp):
            loads = [
                (c.wqkv[:, :], a["w_qkv"]),
                (c.ln[:, 0:1], a["ln1_w"].rearrange("(p o) -> p o", o=1)),
                (c.ln[:, 1:2], a["ln1_b"].rearrange("(p o) -> p o", o=1)),
                (c.ln[:, 2:3], a["ln2_w"].rearrange("(p o) -> p o", o=1)),
                (c.ln[:, 3:4], a["ln2_b"].rearrange("(p o) -> p o", o=1)),
                (c.wq[:, :], a["w_q"]), (c.wk[:, :], a["w_k"]),
            ]
            late = [
                (c.wproj[:, :], a["w_proj"]), (c.wv[:, :], a["w_v"]), (c.wo[:, :], a["w_o"]),
                (c.gate_w[:, :], a["gate_w"]), (c.cos[:, :], a["cos"]), (c.sin[:, :], a["sin"]),
                (c.gate_b[:, :], a["gate_b"].rearrange("(o e) -> o e", o=1).broadcast_to((P, E))),
                (c.w1[:, :].rearrange("p (e n) -> p e n", e=E), a["w1"].rearrange("e p n -> p e n")),
                (c.w2[:, :].rearrange("p (g n) -> p g n", g=E * HT), a["w2"].rearrange("e (k p) n -> p (e k) n", p=P)),
            ]
            c.late_loads = len(late) + NBLK // 8
            for b in range(B):
                sp.dma_start(cols(c.X, b * S, S).rearrange("p (t d) -> p t d", t=QT),
                             a["x"][b].rearrange("(t p) d -> p t d", p=P)).then_inc(s.x, 16)
            for dst, src in loads:
                sp.dma_start(dst, src).then_inc(s.weights, 16)
            for dst, src in late:
                sp.dma_start(dst, src).then_inc(c.late, 16)
            sp.wait_ge(s.zeroed, 1)
            for k in range(NBLK // 8):
                sp.dma_start(c.sorted_x[k * 8 * P:(k + 1) * 8 * P, :].rearrange("(p r) d -> p (r d)", p=P),
                             c.N[:, 0:8 * D]).then_inc(c.late, 16)
            sp.wait_ge(s.x, 16 * B)

        @block.gpsimd
        def _(pool):
            nc.gpsimd.memset(c.ident[:, :], 0.0)
            nc.gpsimd.memset(c.upper[:, :], 1.0)
            nc.gpsimd.memset(c.ones[:, :], 1.0).then_inc(s.spread, 1)
            pool.wait_ge(s.spread, 1)
            nc.gpsimd.affine_select(out=c.ident[:, :], in_=c.ident[:, :], compare_op=ALU.not_equal, fill=1.0,
                                    base=0, pattern=[[-1, P]], channel_multiplier=1)
            nc.gpsimd.affine_select(out=c.upper[:, :], in_=c.upper[:, :], compare_op=ALU.is_gt, fill=0.0,
                                    base=0, pattern=[[1, P]], channel_multiplier=-1)
            nc.gpsimd.iota(c.blocks_i[:, :], pattern=[[1, NBLK]], base=0, channel_multiplier=0)
            nc.gpsimd.iota(c.thresh_i[:, :], pattern=[[P, NT]], base=0, channel_multiplier=0)
            nc.gpsimd.iota(c.down_i[:, :], pattern=[[-1, E]], base=E, channel_multiplier=0).then_inc(s.spread, 1)

        @block.vector
        def _(dve):
            nc.vector.memset(c.N[:, 0:8 * D], 0.0).then_inc(s.zeroed, 1)
            nc.vector.memset(c.zero_rows[:, :], 0.0)
            nc.vector.memset(c.reset[:, :], 1.0).then_inc(s.swapped, 1)
            nc.vector.memset(c.vstage[:, :], 1.0)
            nc.vector.memset(c.bank[7], 0.0)
            dve.wait_ge(s.swapped, 1)
            nc.vector.memset(c.reset[:, :].rearrange("p (e t) -> p e t", e=E)[:, :, 0:1], 0.0)
            dve.wait_ge(s.spread, 2)
            nc.vector.tensor_copy(c.blocks[:, :], c.blocks_i[:, :])
            nc.vector.tensor_copy(c.thresh[:, :], c.thresh_i[:, :])
            nc.vector.tensor_copy(c.down[:, :], c.down_i[:, :])
            dve.wait_ge(s.weights, 16 * 7)
            for w, sw in ((c.wq, c.wq_sw), (c.wk, c.wk_sw)):
                wv = w[:, :].rearrange("p (h t c) -> p h t c", t=2, c=HD // 2)
                sv = sw[:, :].rearrange("p (h t c) -> p h t c", t=2, c=HD // 2)
                for t in range(2):
                    ins = nc.vector.tensor_copy(sv[:, :, t, :], wv[:, :, 1 - t, :])
            ins.then_inc(s.swapped, 1)


def gather_outputs(pool, c, b, gathered):
    for t in range(QT * b, QT * (b + 1)):
        pool.indirect_dma_start(
            c.N[:, t * D:(t + 1) * D], None,
            c.sorted_y[:, :], bass.IndirectOffsetOnAxis(ap=c.pos[:, t:t + 1], axis=0)).then_inc(gathered, 16)


def combine(dve, c, s, b, gathered, count):
    dve.wait_ge(gathered, count)
    n, y, x = (cols(v, b * S, S) for v in (c.N, c.Y, c.X))
    c.nc.vector.tensor_tensor(n, n, y, ALU.add).then_inc(s.summed, 1)
    dve.wait_ge(s.summed, b + 1)
    c.nc.vector.scalar_tensor_tensor(out=x, in0=n, scalar=0.5, in1=x, op0=ALU.mult, op1=ALU.add)\
        .then_inc(s.combined, 1)


def project(nc, c, stage, ffn, gather):
    rows_k = P if ffn else KV * HD
    norms = 2 if ffn else 1
    with ExitStack() as ctx:
        s = sems(ctx, nc, f"p{stage}", "ln held var std transposed zT qk_ready v_ready "
                 "hi lo v_staged stored:2 rot v_stored gathered summed combined rings")
        block = ctx.enter_context(nc.Block())
        w = c.work
        n_sb, zT = w[:, 0:512], w[:, 512:1024]
        hi = [w[:, 1024:1536], w[:, 1536:2048]]
        lo = [w[:, 2048:2560], w[:, 2560:3072]]
        rot = [w[:, 3072:3584], w[:, 3584:4096]]
        rot2 = [w[:, 4096:4608], w[:, 4608:5120]]
        T, qkp, vp, swp = c.bank[0], [c.bank[1], c.bank[2]], c.bank[3], [c.bank[4], c.bank[5]]
        rows = [P, rows_k]
        if ffn:
            wts = [c.wqkv[:, 0:D], c.wqkv[:, D:2 * D]]
            wv = c.wqkv[:, 2 * D:3 * D]
        else:
            wts = [c.wq[:, :], c.wk[:, :]]
            wv = c.wv[:, :]
        wsw = [c.wq_sw[:, :], c.wk_sw[:, :]]

        @block.gpsimd
        def _(pool):
            if gather:
                for b in range(B):
                    gather_outputs(pool, c, b, s.gathered)
                    pool.wait_ge(s.gathered, 16 * QT * (b + 1))
            if stage == 0:
                nc.gpsimd.memset(c.Q[:, :].bitcast(F32), 0.0)
                nc.gpsimd.memset(c.K[:, :].bitcast(F32), 0.0).then_inc(s.rings, 1)
                pool.wait_ge(s.rings, 1)
                nc.gpsimd.memset(c.K[MROW:MROW + 2, :].bitcast(F32), -1.0)

        @block.vector
        def _(dve):
            def norm(b):
                if gather:
                    combine(dve, c, s, b, s.gathered, 16 * QT * (b + 1))
                    dve.wait_ge(s.combined, b + 1)
                if ffn:
                    layer_norm(dve, c, s, b * 8, lambda t: cols(c.X, b * S + t * D, D),
                               lambda t: cols(c.Y, b * S + t * D, D), s.var, s.std, 2 * b)
                    wait(dve, s.transposed, b)
                    layer_norm(dve, c, s, b * 8 + 4, lambda t: cols(c.Y, b * S + t * D, D),
                               lambda t: n_sb[:, t * D:(t + 1) * D], s.var, s.std, 2 * b + 1)
                else:
                    wait(dve, s.transposed, b)
                    layer_norm(dve, c, s, b * 4, lambda t: cols(c.X, b * S + t * D, D),
                               lambda t: n_sb[:, t * D:(t + 1) * D], s.var, s.std, b)

            def low_parts(b):
                if not ffn:
                    for i in range(2):
                        r = rows[i]
                        dve.wait_ge(s.qk_ready, 2 * b + i + 1)
                        wait(dve, s.lo, 2 * b)
                        nc.vector.tensor_tensor(rot[i][0:r, :], qkp[i][0:r, :], c.cos[0:r, :], ALU.mult)
                        nc.vector.tensor_tensor(rot2[i][0:r, :], swp[i][0:r, :], c.sin[0:r, :], ALU.mult).then_inc(s.rot, 1)
                    for i in range(2):
                        r = rows[i]
                        dve.wait_ge(s.rot, 4 * b + i + 1)
                        nc.vector.tensor_tensor(rot[i][0:r, :], rot[i][0:r, :], rot2[i][0:r, :], ALU.add).then_inc(s.rot, 1)
                for i in range(2):
                    r = rows[i]
                    dve.wait_ge(s.hi, 2 * b + i + 1)
                    wait(dve, s.stored[i], 16 * 2 * b)
                    full = qkp[i] if ffn else rot[i]
                    nc.vector.tensor_tensor(lo[i][0:r, :].bitcast(F32R), full[0:r, :], hi[i][0:r, :],
                                            ALU.subtract).then_inc(s.lo, 1)

            norm(0)
            for b in (0,):
                norm(b + 1)
                low_parts(b)
            with dve.Fori(1, B - 1) as b:
                norm(b + 1)
                low_parts(b)
            low_parts(B - 1)

        @block.scalar
        def _(act):
            def roots(b):
                for k in range(norms):
                    square_root(act, c, s.var, s.std, norms * b + k)

            def evacuate(b, last=False):
                act.wait_ge(s.transposed, b + 1)
                wait(act, s.v_ready, b)
                if ffn:
                    nc.scalar.activation(zT, T[:, :], ACT.Identity, bias=c.ln[:, 1:2],
                                         scale=c.ln[:, 0:1]).then_inc(s.zT, 1)
                else:
                    nc.scalar.activation(zT, T[:, :], ACT.Copy).then_inc(s.zT, 1)
                if not last:
                    roots(b + 1)
                for i in range(2):
                    r = rows[i]
                    wait(act, s.stored[i], 16 * 2 * b)
                    if ffn:
                        act.wait_ge(s.qk_ready, 2 * b + i + 1)
                        full = qkp[i]
                    else:
                        act.wait_ge(s.rot, 4 * b + i + 3)
                        full = rot[i]
                    nc.scalar.activation(hi[i][0:r, :].bitcast(F32R), full[0:r, :], ACT.Copy).then_inc(s.hi, 1)
                act.wait_ge(s.v_ready, b + 1)
                wait(act, s.stored[0], 16 * 2 * b)
                wait(act, s.v_staged, b * QT)
                wait(act, s.v_stored, 16 * b)
                vs = c.vstage[:, :].rearrange("p (g k j e) -> p g k j e", g=G, k=QT, j=J)
                for t in range(QT):
                    src = vp[:, t * P:t * P + (D if ffn else KV * HD)]
                    if ffn:
                        src = src.rearrange("p (g j d) -> p g j d", g=G, j=J)
                    else:
                        src = src.rearrange("p (g j d) -> p g j d", g=G, j=1).broadcast_to((P, G, J, HD))
                    nc.scalar.activation(vs[:, :, t, :, 0:HD], src, ACT.Copy).then_inc(s.v_staged, 1)

            roots(0)
            evacuate(0)
            with act.Fori(1, B - 1) as b:
                evacuate(b)
            evacuate(B - 1, last=True)

        @block.tensor
        def _(pe):
            def body(b):
                pe.wait_ge(s.ln, b * 4 * norms + 4 * norms)
                wait(pe, s.zT, b)
                for t in range(QT):
                    ins = nc.tensor.transpose(T[:, t * P:(t + 1) * P], n_sb[:, t * D:(t + 1) * D], c.ident[:, :])
                ins.then_inc(s.transposed, 1)
                pe.wait_ge(s.zT, b + 1)
                wait(pe, s.lo, 2 * b)
                for i in range(2):
                    if not ffn:
                        nc.tensor.matmul(swp[i][0:rows[i], :], wsw[i], zT, start=True, stop=True)
                    nc.tensor.matmul(qkp[i][0:rows[i], :], wts[i], zT, start=True, stop=True).then_inc(s.qk_ready, 1)
                wait(pe, s.v_staged, b * QT)
                nv = D if ffn else KV * HD
                for t in range(QT):
                    ins = nc.tensor.matmul(vp[:, t * P:t * P + nv], zT[:, t * P:(t + 1) * P], wv, start=True, stop=True)
                ins.then_inc(s.v_ready, 1)

            batches(pe, body)

        @block.sync
        def _(sp):
            def body(b):
                for i in range(2):
                    sp.wait_ge(s.hi, 2 * b + i + 1)
                    sp.dma_start(c.qk_scratch[bass.ds(b * 4 + 2 * i, 1), 0:rows[i], :].rearrange("o r n -> (o r) n"),
                                 hi[i][0:rows[i], :]).then_inc(s.stored[i], 16)
                    sp.wait_ge(s.lo, 2 * b + i + 1)
                    sp.dma_start(c.qk_scratch[bass.ds(b * 4 + 2 * i + 1, 1), 0:rows[i], :].rearrange("o r n -> (o r) n"),
                                 lo[i][0:rows[i], :]).then_inc(s.stored[i], 16)
                sp.wait_ge(s.v_staged, (b + 1) * QT)
                sp.dma_start(c.v_scratch[bass.ds(b * G, G), :, :].rearrange("g p n -> p g n"),
                             c.vstage[:, :].rearrange("p (g n) -> p g n", g=G)).then_inc(s.v_stored, 16)

            batches(sp, body)
            for i in range(2):
                sp.wait_ge(s.stored[i], 32 * B)
            sp.wait_ge(s.v_stored, 16 * B)
            if stage == 0:
                sp.wait_ge(c.late, 16 * c.late_loads)


class Ring:
    BANKS = 3
    PROLOGUE = 33
    STEP = 18

    def __init__(self):
        self.base, self.first, self.n = 0, 0, 0

    @classmethod
    def before(cls, n):
        if isinstance(n, int) and n == 0:
            return cls.PROLOGUE
        return cls.PROLOGUE - 1 + cls.STEP * n

    def batch(self, b):
        if not isinstance(b, int) or b:
            self.base, self.first, self.n = self.before(G * b), (self.PROLOGUE - 1) % self.BANKS, 0

    def turn(self):
        n = self.n
        self.n += 1
        return self.base + n, (self.first + n) % self.BANKS


def attend(nc, c, stage, ffn):
    with ExitStack() as ctx:
        s = sems(ctx, nc, f"t{stage}", "filled freed max_hi max_rows:4 loaded:4 v_loaded:4 "
                 "scores probs pv out_copied recip")
        block = ctx.enter_context(nc.Block())
        LOADS = 9
        ring = [c.bank[0], c.bank[1], c.bank[2]]
        scp = [c.pair[0], c.pair[1]]
        outp = c.bank[7]
        prob = c.work[:, :].rearrange("p (r j n) -> p r j n", r=4, j=J)
        q4 = c.Q[:, :].rearrange("p (s j n) -> p s j n", s=4, j=J)
        k4 = c.K[:, :].rearrange("p (s j n) -> p s j n", s=4, j=J)
        v4 = c.V[:, :].rearrange("p (s k j e) -> p s k j e", s=4, k=QT, j=J)

        def where(b, g, ahead):
            b2, g2 = b + (g + ahead) // G, (g + ahead) % G
            if isinstance(b, int) and b2 >= B:
                return None
            return b2, g2, G * b2 + g2

        @block.sync
        def _(sp):
            def load(b, g, n):
                wait(sp, s.scores, 8 * (n - 3))
                done = s.loaded[g]
                for i, ring in enumerate((q4, k4)):
                    for part in range(4):
                        hl = part // 2 if i == 0 else part % 2
                        src = c.qk_scratch[bass.ds(b * 4 + 2 * i + hl, 1), :, :]
                        if ffn or i == 0:
                            src = src[:, g * J * HD:(g + 1) * J * HD, :].rearrange("o (j d) n -> (o d) j n", j=J)
                        else:
                            src = src[:, g * HD:(g + 1) * HD, :].rearrange("o (j d) n -> (o d) j n", j=1)\
                                .broadcast_to((HD, J, S))
                        sp.dma_start(ring[part * HD:(part + 1) * HD, g, :, :].bitcast(F32), src).then_inc(done, 16)
                sp.dma_start(c.Q[MROW:MROW + 2, g * SLOT:(g + 1) * SLOT].bitcast(F32), c.zero_rows[:, :]).then_inc(done, 16)

            def rows_of_max(b, g, n):
                if isinstance(n, int) and n == 0:
                    sp.wait_ge(s.freed, 17)
                elif isinstance(n, int) and n == NG - 1:
                    sp.wait_ge(s.freed, Ring.before(n - 1) + 1)
                else:
                    sp.wait_ge(s.freed, Ring.before(n - 1) + 5)
                for i in range(2):
                    sp.dma_start(c.Q[MROW + i:MROW + i + 1, g * SLOT:(g + 1) * SLOT].bitcast(F32).rearrange("o (r n) -> o r n", n=P),
                                 c.maxT[:, (2 * (g % 2) + i) * P:(2 * (g % 2) + i + 1) * P].bitcast(F32))\
                        .then_inc(s.max_rows[g], 16)

            for n in range(3):
                load(0, n, n)
            rows_of_max(0, 0, 0)

            def body(b):
                for g in range(G):
                    ahead = where(b, g, 3)
                    if ahead:
                        load(*ahead)
                    nxt = where(b, g, 1)
                    if nxt:
                        rows_of_max(*nxt)

            batches(sp, body)
            for g in range(G):
                sp.wait_ge(s.max_rows[g], 32 * B)

        @block.gpsimd
        def _(pool):
            def load_v(b, g, n):
                wait(pool, s.pv, 4 * (n - 3))
                pool.dma_start(c.V[:, g * QT * J * V1:(g + 1) * QT * J * V1],
                               c.v_scratch[bass.ds(b * G + g, 1), :, :].rearrange("o p n -> (o p) n"))\
                    .then_inc(s.v_loaded[g], 16)

            for n in range(3):
                load_v(0, n, n)

            def body(b):
                for g in range(G):
                    ahead = where(b, g, 3)
                    if ahead:
                        load_v(*ahead)

            batches(pool, body)

        @block.tensor
        def _(pe):
            turns = Ring()

            def next_bank():
                u, k = turns.turn()
                wait(pe, s.freed, u - Ring.BANKS + 1)
                return ring[k]

            def max_scores(b, g, n, j, qt):
                nc.tensor.matmul(next_bank(), q4[:, g, j, qt * P:(qt + 1) * P], k4[:, g, j, :],
                                 start=True, stop=True).then_inc(s.filled, 1)

            def turn_max(b, g, n):
                wait(pe, s.freed, 16 if isinstance(n, int) and n == 0 else Ring.before(n - 1))
                nc.tensor.transpose(next_bank()[0:16, 0:P], c.maxima[:, 16 * (g % 2):16 * (g % 2) + 16],
                                    c.ident[:, :]).then_inc(s.filled, 1)

            def scores(b, g, n, kt, half):
                w = 2 * (4 * n + kt) + half
                wait(pe, s.probs, w - 1)
                for i in range(2):
                    j = 2 * half + i
                    ins = nc.tensor.matmul(scp[half][:, i * S:(i + 1) * S], k4[:, g, j, kt * P:(kt + 1) * P],
                                           q4[:, g, j, :], start=True, stop=True)
                ins.then_inc(s.scores, 1)

            def weigh(b, g, n, kt):
                pe.wait_ge(s.probs, 2 * (4 * n + kt) + 2)
                if kt == 0:
                    pe.wait_ge(s.v_loaded[g], 16 * (b + 1))
                    wait(pe, s.out_copied, n)
                for j in range(J):
                    ins = nc.tensor.matmul(outp[32 * j:32 * j + V1, :], v4[:, g, kt, j, :], prob[:, kt, j, :],
                                           start=(kt == 0), stop=(kt == QT - 1))
                ins.then_inc(s.pv, 1)

            def turn_out(n):
                bank = next_bank()
                pe.wait_ge(s.out_copied, n + 1)
                for t in range(QT):
                    ins = nc.tensor.transpose(bank[:, t * P:(t + 1) * P], c.outT[:, t * P:(t + 1) * P], c.ident[:, :])
                ins.then_inc(s.filled, 1)

            for n in range(2):
                pe.wait_ge(s.loaded[n], 16 * LOADS)
                for j in range(J):
                    for qt in range(QT):
                        max_scores(0, n, n, j, qt)
                if n == 0:
                    turn_max(0, 0, 0)

            def step(b, g, kt, before):
                n = G * b + g
                ahead = where(b, g, 2)
                if kt == 0:
                    pe.wait_ge(s.max_rows[g], 32 * (b + 1))
                    if ahead:
                        pe.wait_ge(s.loaded[ahead[1]], 16 * LOADS * (ahead[0] + 1))
                    nxt = where(b, g, 1)
                if ahead:
                    max_scores(*ahead, kt, 0)
                scores(b, g, n, kt, 0)
                if ahead:
                    max_scores(*ahead, kt, 1)
                scores(b, g, n, kt, 1)
                if ahead:
                    max_scores(*ahead, kt, 2)
                if before:
                    weigh(*before)
                if ahead:
                    max_scores(*ahead, kt, 3)
                if kt == 0 and nxt:
                    turn_max(*nxt)
                if kt == 2 and not (isinstance(b, int) and n == 0):
                    turn_out(n - 1)

            def body(b):
                turns.batch(b)
                for g in range(G):
                    for kt in range(QT):
                        if kt:
                            before = (b, g, G * b + g, kt - 1)
                        elif g:
                            before = (b, g - 1, G * b + g - 1, QT - 1)
                        elif isinstance(b, int) and b == 0:
                            before = None
                        else:
                            before = (b - 1, G - 1, G * b - 1, QT - 1)
                        step(b, g, kt, before)

            batches(pe, body)
            weigh(B - 1, G - 1, NG - 1, QT - 1)
            turn_out(NG - 1)

        @block.scalar
        def _(act):
            def copy_out(n):
                act.wait_ge(s.pv, 4 * n + 4)
                if isinstance(n, int) and n == 0:
                    pass
                elif isinstance(n, int) and n >= NG - 1:
                    act.wait_ge(s.freed, Ring.before(NG - 2) + 3)
                elif isinstance(n, int) and n == NG - 2:
                    act.wait_ge(s.freed, Ring.before(NG - 2) + 2)
                else:
                    act.wait_ge(s.freed, Ring.before(n) + 14)
                nc.scalar.activation(c.outT[:, :], outp[:, :], ACT.Copy).then_inc(s.out_copied, 1)

            def body(b):
                for g in range(G):
                    n = G * b + g
                    for kt in range(QT):
                        if kt == 1 and not (isinstance(b, int) and n == 0):
                            copy_out(n - 1)
                        for half in range(2):
                            t = 4 * n + kt
                            act.wait_ge(s.scores, 2 * t + half + 1)
                            wait(act, s.pv, t - 3)
                            nc.scalar.activation(prob[:, kt, 2 * half:2 * half + 2, :], scp[half][:, :]
                                                 .rearrange("p (j n) -> p j n", j=2), ACT.Exp,
                                                 scale=SCALE).then_inc(s.probs, 1)

            batches(act, body)
            copy_out(NG - 1)

        @block.vector
        def _(dve):
            turns = Ring()

            def next_bank():
                u, k = turns.turn()
                dve.wait_ge(s.filled, u + 1)
                return ring[k]

            def take_max(b, g, n, j, qt):
                k = 16 * (g % 2) + 4 * j + qt
                nc.vector.tensor_reduce(c.maxima[:, k:k + 1], next_bank(), AX.X, ALU.max).then_inc(s.freed, 1)

            def split_max(b, g, n):
                if isinstance(n, int):
                    if n >= 2:
                        dve.wait_ge(s.max_rows[(n - 2) % 4], 32 * ((n - 2) // 4 + 1))
                elif g >= 2:
                    dve.wait_ge(s.max_rows[g - 2], 32 * (b + 1))
                else:
                    dve.wait_ge(s.max_rows[g + 2], 32 * b)
                bank = next_bank()
                hi = c.maxT[:, 2 * (g % 2) * P:(2 * (g % 2) + 1) * P]
                lo = c.maxT[:, (2 * (g % 2) + 1) * P:(2 * (g % 2) + 2) * P]
                nc.vector.tensor_copy(hi, bank[0:16, 0:P]).then_inc(s.max_hi, 1)
                dve.wait_ge(s.max_hi, n + 1)
                nc.vector.tensor_tensor(lo, bank[0:16, 0:P], hi.bitcast(F32), ALU.subtract).then_inc(s.freed, 1)

            def normalise(b, g, n):
                turned = next_bank().rearrange("p (t j r) -> p t j r", t=QT, j=J)
                rec = c.recip[:, :].rearrange("p (t j) -> p t j", t=QT)
                nc.vector.reciprocal(rec, turned[:, :, :, HD]).then_inc(s.recip, 1)
                dve.wait_ge(s.recip, n + 1)
                dst = cols(c.N, b * S, S).rearrange("p (t g j d) -> p t g j d", t=QT, g=G, j=J)[:, :, g, :, :]
                nc.vector.tensor_tensor(dst, turned[:, :, :, 0:HD],
                                        rec.rearrange("p t (j o) -> p t j o", o=1).broadcast_to((P, QT, J, HD)),
                                        ALU.mult).then_inc(s.freed, 1)

            for n in range(2):
                for j in range(J):
                    for qt in range(QT):
                        take_max(0, n, n, j, qt)
                if n == 0:
                    split_max(0, 0, 0)

            def body(b):
                turns.batch(b)
                for g in range(G):
                    n = G * b + g
                    ahead, nxt = where(b, g, 2), where(b, g, 1)
                    for kt in range(QT):
                        if ahead:
                            for qt in range(QT):
                                take_max(*ahead, kt, qt)
                        if kt == 0 and nxt:
                            split_max(*nxt)
                        if kt == 2 and not (isinstance(b, int) and n == 0):
                            if g:
                                normalise(b, g - 1, n - 1)
                            else:
                                normalise(b - 1, G - 1, n - 1)

            batches(dve, body)
            normalise(B - 1, G - 1, NG - 1)


def finish_attention(nc, c, stage, ffn):
    with ExitStack() as ctx:
        s = sems(ctx, nc, f"o{stage}", "staged turned aT proj added ln held var std nT uT logit logged kept")
        block = ctx.enter_context(nc.Block())
        w = c.work
        a_sb, aT, n_sb, uT = w[:, 0:512], w[:, 512:1024], w[:, 1024:1536], w[:, 1536:2048]
        T, pp, T2, lp = c.bank[0], c.bank[1], c.bank[2], c.bank[3]
        weight = c.wproj if ffn else c.wo
        res = c.Y if ffn else c.X

        def ahead(eng, body):
            body(0, True)
            with eng.Fori(1, B - 1) as b:
                body(b, True)
            body(B - 1, False)

        @block.gpsimd
        def _(pool):
            def stage_in(b):
                wait(pool, s.turned, b)
                nc.gpsimd.tensor_copy(a_sb, cols(c.N, b * S, S)).then_inc(s.staged, 1)

            stage_in(0)
            stage_in(1)
            with pool.Fori(1, B - 1) as b:
                stage_in(b + 1)

        @block.tensor
        def _(pe):
            def project_out(b):
                pe.wait_ge(s.staged, b + 1)
                wait(pe, s.aT, b)
                for t in range(QT):
                    ins = nc.tensor.transpose(T[:, t * P:(t + 1) * P], a_sb[:, t * P:(t + 1) * P], c.ident[:, :])
                ins.then_inc(s.turned, 1)
                pe.wait_ge(s.aT, b + 1)
                wait(pe, s.added, b)
                for t in range(QT):
                    ins = nc.tensor.matmul(pp[:, t * P:(t + 1) * P], aT[:, t * P:(t + 1) * P], weight[:, :],
                                           start=True, stop=True)
                ins.then_inc(s.proj, 1)

            def gate(b):
                pe.wait_ge(s.ln, 4 * b + 4)
                wait(pe, s.uT, b)
                for t in range(QT):
                    ins = nc.tensor.transpose(T2[:, t * P:(t + 1) * P], n_sb[:, t * P:(t + 1) * P], c.ident[:, :])
                ins.then_inc(s.nT, 1)
                pe.wait_ge(s.uT, b + 1)
                wait(pe, s.logged, b)
                for t in range(QT):
                    ins = nc.tensor.matmul(lp[:, t * E:(t + 1) * E], uT[:, t * P:(t + 1) * P], c.gate_w[:, :],
                                           start=True, stop=True)
                ins.then_inc(s.logit, 1)

            def body(b, more):
                if more:
                    project_out(b + 1)
                if ffn:
                    gate(b)

            project_out(0)
            ahead(pe, body)

        @block.scalar
        def _(act):
            def copy_in(b):
                act.wait_ge(s.turned, b + 1)
                wait(act, s.proj, b)
                nc.scalar.activation(aT, T[:, :], ACT.Copy).then_inc(s.aT, 1)

            def body(b, more):
                if more:
                    copy_in(b + 1)
                if ffn:
                    square_root(act, c, s.var, s.std, b)
                    act.wait_ge(s.nT, b + 1)
                    wait(act, s.logit, b)
                    nc.scalar.activation(uT, T2[:, :], ACT.Identity, bias=c.ln[:, 3:4],
                                         scale=c.ln[:, 2:3]).then_inc(s.uT, 1)
                    nc.scalar.activation(cols(c.N, b * S, S), n_sb, ACT.Copy).then_inc(s.kept, 1)

            copy_in(0)
            ahead(act, body)

        @block.vector
        def _(dve):
            def add(b):
                dve.wait_ge(s.proj, b + 1)
                nc.vector.tensor_tensor(cols(res, b * S, S), pp[:, :], cols(res, b * S, S), ALU.add).then_inc(s.added, 1)

            def add_gate_bias(b):
                dve.wait_ge(s.logit, b + 1)
                nc.vector.tensor_tensor(
                    cols(c.logits, b * QT * E, QT * E).rearrange("p (t e) -> p t e", t=QT),
                    lp[:, 0:QT * E].rearrange("p (t e) -> p t e", t=QT),
                    c.gate_b[:, :].rearrange("p (o e) -> p o e", o=1).broadcast_to((P, QT, E)),
                    ALU.add).then_inc(s.logged, 1)

            def body(b, more):
                if ffn:
                    dve.wait_ge(s.added, b + 1)
                    wait(dve, s.nT, b)
                    wait(dve, s.kept, b)
                    layer_norm(dve, c, s, 4 * b, lambda t: cols(c.Y, b * S + t * D, D),
                               lambda t: n_sb[:, t * D:(t + 1) * D], s.var, s.std, b)
                if more:
                    add(b + 1)
                if ffn and not (isinstance(b, int) and b == 0):
                    add_gate_bias(b - 1)

            add(0)
            ahead(dve, body)
            if ffn:
                add_gate_bias(B - 1)


def route(nc, c, stage):
    with ExitStack() as ctx:
        s = sems(ctx, nc, f"r{stage}", "chain onehot counted positions scattered")
        block = ctx.enter_context(nc.Block())
        TE = NT * E
        w = c.work
        mask, val, onehot = w[:, 0:TE], w[:, TE:2 * TE], w[:, 2 * TE:3 * TE]
        tot, inc, off = w[:, 3 * TE:4 * TE], w[:, 4 * TE:5 * TE], w[:, 5 * TE:6 * TE]
        big = w[:, 2048:2048 + NBLK * E]
        small = w[:, 3072:3072 + 256]
        best, top = small[:, 0:NT], small[:, NT:2 * NT]
        nblk, ends, base = small[:, 64:72], small[:, 72:80], small[:, 80:88]
        blk, posf, ones8 = small[:, 96:96 + NBLK], small[:, 160:192], small[:, 200:208]
        rank_ps, tot_ps = c.bank[0], c.bank[1]

        def te(x):
            return x.rearrange("p (t e) -> p t e", e=E)

        def et(x):
            return x.rearrange("p (e t) -> p e t", e=E)

        def inner(x, n):
            return x.rearrange("p (a o) -> p a o", o=1).broadcast_to((P, x.shape[1], n))

        def outer(x, n):
            return x.rearrange("p (o a) -> p o a", o=1).broadcast_to((P, n, x.shape[1]))

        @block.vector
        def _(dve):
            links = [0]

            def link(ins):
                links[0] += 1
                ins.then_inc(s.chain, 1)
                dve.wait_ge(s.chain, links[0])

            lg = te(c.logits[:, :])
            link(nc.vector.tensor_reduce(top, lg, AX.X, ALU.max))
            link(nc.vector.tensor_tensor(te(mask), lg, inner(top, E), ALU.is_equal))
            link(nc.vector.tensor_tensor(te(val), te(mask), outer(c.down[:, :], NT), ALU.mult))
            link(nc.vector.tensor_reduce(best, te(val), AX.X, ALU.max))
            nc.vector.memset(ones8, 1.0)
            nc.vector.tensor_tensor(te(onehot), te(val), inner(best, E), ALU.is_equal).then_inc(s.onehot, 1)
            dve.wait_ge(s.counted, 2)
            link(nc.vector.tensor_copy(et(tot), te(tot_ps[:, 0:TE]).rearrange("p t e -> p e t")))
            link(nc.vector.tensor_tensor_scan(inc, c.reset[:, :], tot, 0.0, ALU.mult, ALU.add))
            link(nc.vector.tensor_tensor(off, inc, tot, ALU.subtract))
            cnt = et(inc)[:, :, NT - 1]
            link(nc.vector.tensor_tensor(et(mask), cnt.rearrange("p (e o) -> p e o", o=1).broadcast_to((P, E, NT)),
                                         outer(c.thresh[:, :], E), ALU.is_gt))
            link(nc.vector.tensor_reduce(nblk, et(mask), AX.X, ALU.add))
            link(nc.vector.tensor_tensor_scan(ends, ones8, nblk, 0.0, ALU.mult, ALU.add))
            link(nc.vector.tensor_tensor(base, ends, nblk, ALU.subtract))
            link(nc.vector.tensor_scalar(base, base, float(P), None, ALU.mult))
            link(nc.vector.tensor_tensor(et(off), et(off), inner(base, NT), ALU.add))
            link(nc.vector.tensor_tensor(te(val), te(rank_ps[:, 0:TE]), et(off).rearrange("p e t -> p t e"), ALU.add))
            link(nc.vector.tensor_tensor(te(val), te(val), te(onehot), ALU.mult))
            link(nc.vector.tensor_reduce(posf, te(val), AX.X, ALU.add))
            nc.vector.tensor_copy(c.pos[:, :], posf).then_inc(s.positions, 1)
            bg = big.rearrange("p (b e) -> p b e", e=E)
            link(nc.vector.tensor_tensor(bg, inner(c.blocks[:, :], E), outer(ends, NBLK), ALU.is_ge))
            link(nc.vector.tensor_reduce(blk, bg, AX.X, ALU.add))
            link(nc.vector.tensor_scalar(blk, blk, float(E - 1), float(HID), ALU.min, ALU.mult))
            link(nc.vector.tensor_copy(c.expert_at[:, :], blk[0:1, :]))

        @block.tensor
        def _(pe):
            pe.wait_ge(s.onehot, 1)
            nc.tensor.matmul(rank_ps[:, 0:TE], c.upper[:, :], onehot, start=True, stop=True).then_inc(s.counted, 1)
            nc.tensor.matmul(tot_ps[:, 0:TE], c.ones[:, :], onehot, start=True, stop=True).then_inc(s.counted, 1)

        @block.gpsimd
        def _(pool):
            pool.wait_ge(s.positions, 1)
            for t in range(NT):
                nc.gpsimd.indirect_dma_start(
                    c.sorted_x[:, :], bass.IndirectOffsetOnAxis(ap=c.pos[:, t:t + 1], axis=0),
                    c.N[:, t * D:(t + 1) * D], None).then_inc(s.scattered, 16)
            pool.wait_ge(s.scattered, 16 * NT)


def experts(nc, c, stage):
    with ExitStack() as ctx:
        s = sems(ctx, nc, f"e{stage}", "loaded:4 turned uT hidden gelu hidden_turned hT out out_copied stored:4")
        block = ctx.enter_context(nc.Block())
        w = c.work
        ring = 4
        turns = NBLK // ring
        x_sb = [w[:, i * 128:(i + 1) * 128] for i in range(ring)]
        uT = [w[:, 512:640], w[:, 640:768]]
        h_sb = [w[:, 1024:1536], w[:, 1536:2048]]
        hT = [w[:, 2048:2560], w[:, 2560:3072]]
        y_sb = [w[:, 3072 + i * 128:3200 + i * 128] for i in range(ring)]
        Tp, hp, hTp, yp = [c.bank[0], c.bank[1]], [c.bank[2], c.bank[3]], [c.bank[4], c.bank[5]], [c.bank[6], c.bank[7]]

        def blocks(eng, step):
            for r in range(ring):
                step(r, r, 0)
            with eng.Fori(0, (turns - 2) // 2) as pair:
                for turn in range(2):
                    for r in range(ring):
                        step(ring * 2 * pair + ring * (turn + 1) + r, r, 2 * pair + (turn + 1))
            for r in range(ring):
                step(NBLK - ring + r, r, turns - 1)

        def exists(i):
            return not isinstance(i, int) or i < NBLK

        @block.sync
        def _(sp):
            def load(i, r, k):
                wait(sp, s.turned, i - ring + 1)
                sp.dma_start(x_sb[r], c.sorted_x[bass.ds(i * P, P), :]).then_inc(s.loaded[r], 16)

            def step(i, r, k):
                if exists(i + 3):
                    load(i + 3, (r + 3) % ring, k)

            for i in range(3):
                load(i, i, 0)
            blocks(sp, step)

        @block.gpsimd
        def _(pool):
            def step(i, r, k):
                pool.wait_ge(s.out_copied, i + 1)
                pool.dma_start(c.sorted_y[bass.ds(i * P, P), :], y_sb[r]).then_inc(s.stored[r], 16)

            blocks(pool, step)
            for r in range(ring):
                pool.wait_ge(s.stored[r], 16 * NBLK // ring)

        @block.tensor
        def _(pe):
            def turn(i, r, k):
                pe.wait_ge(s.loaded[r], 16 * (k + 1))
                wait(pe, s.uT, i - 1)
                nc.tensor.transpose(Tp[r % 2][:, 0:P], x_sb[r], c.ident[:, :]).then_inc(s.turned, 1)

            def hidden(i, par, at):
                pe.wait_ge(s.uT, i + 1)
                wait(pe, s.gelu, i - 1)
                nc.tensor.matmul(hp[par][:, :], uT[par], cols(c.w1, at, HID), start=True, stop=True).then_inc(s.hidden, 1)

            def turn_hidden(i, par):
                pe.wait_ge(s.gelu, i + 1)
                wait(pe, s.hT, i - 1)
                for t in range(HT):
                    ins = nc.tensor.transpose(hTp[par][:, t * P:(t + 1) * P], h_sb[par][:, t * P:(t + 1) * P], c.ident[:, :])
                ins.then_inc(s.hidden_turned, 1)

            def output(i, par, at):
                pe.wait_ge(s.hT, i + 1)
                wait(pe, s.out_copied, i - 1)
                for t in range(HT):
                    ins = nc.tensor.matmul(yp[par][:, 0:D], hT[par][:, t * P:(t + 1) * P], cols(c.w2, at + t * D, D),
                                           start=(t == 0), stop=(t == HT - 1))
                ins.then_inc(s.out, 1)

            def expert(i):
                return pe.value_load(c.expert_at[0:1, bass.ds(i, 1)], min_val=0, max_val=(E - 1) * HID)

            following = [None]

            def step(i, r, k):
                if exists(i + 2):
                    turn(i + 2, (r + 2) % ring, k + (r + 2) // ring)
                turn_hidden(i, r % 2)
                if exists(i + 1):
                    if r == 0:
                        following[0] = expert(i + 1)
                    hidden(i + 1, (r + 1) % 2, following[0])
                own = expert(i)
                if r < ring - 1 and exists(i + 2):
                    following[0] = expert(i + 2)
                output(i, r % 2, own)

            turn(0, 0, 0)
            turn(1, 1, 0)
            hidden(0, 0, expert(0))
            blocks(pe, step)

        @block.scalar
        def _(act):
            def affine(i, par):
                act.wait_ge(s.turned, i + 1)
                wait(act, s.hidden, i - 1)
                nc.scalar.activation(uT[par], Tp[par][:, 0:P], ACT.Identity, bias=c.ln[:, 3:4],
                                     scale=c.ln[:, 2:3]).then_inc(s.uT, 1)

            def gelu(i, par):
                act.wait_ge(s.hidden, i + 1)
                wait(act, s.hidden_turned, i - 1)
                nc.scalar.activation(h_sb[par], hp[par][:, :], ACT.Gelu_apprx_tanh).then_inc(s.gelu, 1)

            def step(i, r, k):
                if exists(i + 2):
                    affine(i + 2, r % 2)
                if exists(i + 1):
                    gelu(i + 1, (r + 1) % 2)

            affine(0, 0)
            affine(1, 1)
            gelu(0, 0)
            blocks(act, step)

        @block.vector
        def _(dve):
            def step(i, r, k):
                dve.wait_ge(s.hidden_turned, i + 1)
                wait(dve, s.out, i - 1)
                nc.vector.tensor_copy(hT[r % 2], hTp[r % 2][:, :]).then_inc(s.hT, 1)
                dve.wait_ge(s.out, i + 1)
                wait(dve, s.stored[r], 16 * k)
                nc.vector.tensor_copy(y_sb[r], yp[r % 2][:, 0:D]).then_inc(s.out_copied, 1)

            blocks(dve, step)


def finish(nc, c, out):
    with ExitStack() as ctx:
        s = sems(ctx, nc, "fin", "gathered:8 summed combined stored")
        block = ctx.enter_context(nc.Block())

        @block.gpsimd
        def _(pool):
            for b in range(B):
                gather_outputs(pool, c, b, s.gathered[b])

        @block.vector
        def _(dve):
            for b in range(B):
                combine(dve, c, s, b, s.gathered[b], 16 * QT)

        @block.sync
        def _(sp):
            for b in range(B):
                sp.wait_ge(s.combined, b + 1)
                sp.dma_start(out[b].rearrange("(t p) d -> p t d", p=P),
                             cols(c.X, b * S, S).rearrange("p (t d) -> p t d", t=QT)).then_inc(s.stored, 16)
            sp.wait_ge(s.stored, 16 * B)


def build(nc, a, out):
    with ExitStack() as ctx:
        def sb(name, shape, dt=F32):
            return ctx.enter_context(nc.sbuf_tensor(name, shape, dt))

        c = Core()
        c.nc = nc
        c.late = ctx.enter_context(nc.semaphore("late"))
        c.X, c.Y, c.N = (sb(n, [P, B * S]) for n in ("X", "Y", "N"))
        c.Q, c.K = sb("Q", [P, 4 * SLOT], F32R), sb("K", [P, 4 * SLOT], F32R)
        c.V = sb("V", [P, 4 * QT * J * V1])
        c.work = sb("work", [P, 4 * SLOT])
        c.outT = sb("outT", [P, S])
        c.w1, c.w2 = sb("w1", [P, E * HID]), sb("w2", [P, E * HID])
        c.wqkv, c.wproj, c.wq, c.wo = sb("wqkv", [P, 3 * D]), sb("wproj", [P, D]), sb("wq", [P, D]), sb("wo", [P, D])
        c.wq_sw, c.wk, c.wk_sw, c.wv = sb("wq_sw", [P, D]), sb("wk", [P, KV * HD]), sb("wk_sw", [P, KV * HD]), sb("wv", [P, KV * HD])
        c.gate_w, c.gate_b, c.ln = sb("gate_w_sb", [P, E]), sb("gate_b_sb", [P, E]), sb("ln", [P, 4])
        c.cos, c.sin = sb("cos_sb", [P, S]), sb("sin_sb", [P, S])
        c.vstage = sb("vstage", [P, G * QT * J * V1])
        c.stats, c.moments = sb("stats", [P, QT, 6]), sb("moments", [P, QT, 2])
        c.vareps, c.std, c.rstd = sb("vareps", [P, QT]), sb("std", [P, QT]), sb("rstd", [P, QT])
        c.ident, c.upper, c.ones = sb("ident", [P, P]), sb("upper", [P, P]), sb("ones", [P, P])
        c.maxima = sb("maxima", [P, 32])
        c.maxT = sb("maxT", [16, 4 * P], F32R)
        c.zero_rows = sb("zero_rows", [2, SLOT])
        c.recip = sb("recip", [P, QT * J])
        c.logits, c.reset = sb("logits", [P, NT * E]), sb("reset", [P, E * NT])
        c.pos, c.expert_at = sb("pos", [P, NT], U32), sb("expert_at", [1, NBLK], U32)
        c.blocks_i, c.thresh_i, c.down_i = sb("blocks_i", [P, NBLK], U32), sb("thresh_i", [P, NT], U32), sb("down_i", [P, E], U32)
        c.blocks, c.thresh, c.down = sb("blocks", [P, NBLK]), sb("thresh", [P, NT]), sb("down", [P, E])
        banks = ctx.enter_context(nc.psum_tensor("banks", [P, 8 * 512], F32))
        c.bank = [banks[:, i * 512:(i + 1) * 512] for i in range(8)]
        c.pair = [banks[:, 3 * 512:5 * 512], banks[:, 5 * 512:7 * 512]]
        c.qk_scratch = nc.dram_tensor("qk_scratch", [B * 4, P, S], F32).ap()
        c.v_scratch = nc.dram_tensor("v_scratch", [B * G, P, QT * J * V1], F32).ap()
        c.sorted_x = nc.dram_tensor("sorted_x", [NBLK * P, D], F32).ap()
        c.sorted_y = nc.dram_tensor("sorted_y", [NBLK * P, D], F32).ap()

        setup(nc, c, a)
        for stage, ffn in enumerate((True, False, True)):
            project(nc, c, stage, ffn, gather=stage == 1)
            attend(nc, c, stage, ffn)
            finish_attention(nc, c, stage, ffn)
            if ffn:
                route(nc, c, stage)
                experts(nc, c, stage)
        finish(nc, c, out)


def rope_tables():
    half = HD // 2
    inv = (np.float32(1.0) / np.float32(10000.0) ** (np.arange(half, dtype=np.float32) * np.float32(2.0) / np.float32(HD)))
    freq = np.arange(S, dtype=np.float32)[None, :] * inv.astype(np.float32)[:, None]
    cos, sin = np.cos(freq).astype(np.float32), np.sin(freq).astype(np.float32)
    return (np.tile(np.concatenate([cos, cos]), (H, 1)), np.tile(np.concatenate([-sin, sin]), (H, 1)))


def kernel(**inputs):
    import concourse.bacc as bacc
    from concourse.bass_utils import run_bass_kernel_spmd

    names = {
        "x": "L0_attn_x", "w_q": "L0_attn_w_q", "w_k": "L0_attn_w_k", "w_v": "L0_attn_w_v", "w_o": "L0_attn_w_o",
        "ln1_w": "L0_ffn_ln1_w", "ln1_b": "L0_ffn_ln1_b", "w_qkv": "L0_ffn_w_qkv", "w_proj": "L0_ffn_w_proj",
        "ln2_w": "L0_ffn_ln2_w", "ln2_b": "L0_ffn_ln2_b", "gate_w": "L0_ffn_gate_w", "gate_b": "L0_ffn_gate_b",
        "w1": "L0_ffn_w1", "w2": "L0_ffn_w2",
    }
    data = {k: np.ascontiguousarray(inputs[v]) for k, v in names.items()}
    data["cos"], data["sin"] = rope_tables()
    nc = bacc.Bacc("TRN2", target_bir_lowering=False, num_devices=1)
    arrays, args = {}, {}
    for k, v in data.items():
        arrays[f"in_{k}"] = v
        args[k] = nc.dram_tensor(f"in_{k}", v.shape, mybir.dt.from_np(v.dtype), kind="ExternalInput").ap()
    out = nc.dram_tensor("out_x", (B, S, D), F32, kind="ExternalOutput").ap()
    build(nc, args, out)
    r = run_bass_kernel_spmd(nc, [arrays], core_ids=[0])
    return r.results[0]["out_x"]
```
